# Optimizing a Trainium2 kernel written in Bass

```python
import numpy as np
import jax
import jax.numpy as jnp

def _softmax(x, axis=-1):
    return jax.nn.softmax(x, axis=axis)

def _gelu(x):
    return jax.nn.gelu(x, approximate=True)

def _silu(x):
    return jax.nn.silu(x)

def _sigmoid(x):
    return jax.nn.sigmoid(x)

def _layernorm(x, axis=-1, eps=1e-05):
    m = jnp.mean(x, axis=axis, keepdims=True)
    v = jnp.var(x, axis=axis, keepdims=True)
    return (x - m) / jnp.sqrt(v + eps)

def _scatter_add(tgt, idx, src, axis=0):
    return tgt.at[idx].add(src)

def _segment_sum(src, seg, n):
    return jax.ops.segment_sum(src, seg, n)
kernel_name = 'mk_adj_preln_d2_adj_r2_d39924'

def setup_inputs(seed: int=0):
    np.random.seed(seed)
    _w = jnp.asarray

    def _rec_inputs():
        import jax
        import jax.numpy as jnp
        _gk = jax.random.key(seed)
        x = -0.0003929 + 0.9999 * jax.random.normal(jax.random.fold_in(_gk, 1), (32, 256, 512), jnp.float32)
        _a = jax.random.bernoulli(jax.random.fold_in(_gk, 2), 0.015625, (256, 256))
        _a = jnp.logical_or(_a, jnp.swapaxes(_a, -1, -2))
        _a = jnp.logical_or(_a, jnp.eye(256, dtype=bool))
        _af = _a.astype(jnp.float32)
        _af = _af * jax.random.uniform(jax.random.fold_in(_gk, 3), (256, 256), jnp.float32, 0.05, 0.198159)
        adj = _af
        return (x, adj)
    x, adj = _rec_inputs()

    def _L0_gnn_setup():
        import jax, jax.numpy as jnp
        import numpy as np
        NEG_SLOPE = 0.01
        key = jax.random.key(seed)
        k1, k2, k3, k4, k5 = jax.random.split(key, 5)
        B, C, N, O = (32, 256, 512, 256)
        x = jax.random.normal(k1, (B, C, N), dtype=jnp.float32)
        wq = jax.random.normal(k2, (C,), dtype=jnp.float32) * (1.0 / np.sqrt(C))
        wk = jax.random.normal(k3, (C,), dtype=jnp.float32) * (1.0 / np.sqrt(C))
        wm = jax.random.normal(k4, (O, C), dtype=jnp.float32) * (1.0 / np.sqrt(C))
        bm = jax.random.normal(k5, (O,), dtype=jnp.float32) * 0.01
        return {'x': x, 'wq': wq, 'wk': wk, 'wm': wm, 'bm': bm}
    _L0_gnn_all = _L0_gnn_setup()
    _L0_gnn_in = {k: v for k, v in _L0_gnn_all.items() if k in ('wq', 'wk', 'bm')}
    del _L0_gnn_all

    def _L1_gnn_setup():
        import jax, jax.numpy as jnp
        import numpy as np
        EPS = 1e-08

        def _row_stochastic_causal(A, causal_mask):
            A = A * causal_mask
            deg = jnp.maximum(A.sum(axis=-1, keepdims=True), EPS)
            return A / deg
        key = jax.random.key(seed)
        k = jax.random.split(key, 5)
        B, N, D = (4, 1024, 512)
        s = 1.0 / np.sqrt(D)
        h = jax.random.normal(k[0], (B, N, D), dtype=jnp.float32)
        W_lang = jax.random.normal(k[1], (D, D), dtype=jnp.float32) * s
        W_grav = jax.random.normal(k[2], (D, D), dtype=jnp.float32) * s
        W_V = jax.random.normal(k[3], (D, D), dtype=jnp.float32) * s
        W_O = jax.random.normal(k[4], (D, D), dtype=jnp.float32) * s
        causal_mask = jnp.tril(jnp.ones((N, N), dtype=jnp.float32))
        gate_logit = jnp.zeros((), jnp.float32)
        log_sigma = jnp.zeros((), jnp.float32)
        return {'h': h, 'causal_mask': causal_mask, 'W_lang': W_lang, 'W_grav': W_grav, 'W_V': W_V, 'W_O': W_O, 'gate_logit': gate_logit, 'log_sigma': log_sigma}
    _L1_gnn_all = _L1_gnn_setup()
    _L1_gnn_in = {k: v for k, v in _L1_gnn_all.items() if k in ('W_lang', 'W_grav', 'W_V', 'W_O', 'gate_logit', 'log_sigma')}
    del _L1_gnn_all
    return {'x': x, 'adj': adj, 'L0_gnn_wq': _L0_gnn_in['wq'], 'L0_gnn_wk': _L0_gnn_in['wk'], 'L0_gnn_bm': _L0_gnn_in['bm'], 'L1_gnn_W_lang': _L1_gnn_in['W_lang'], 'L1_gnn_W_grav': _L1_gnn_in['W_grav'], 'L1_gnn_W_V': _L1_gnn_in['W_V'], 'L1_gnn_W_O': _L1_gnn_in['W_O'], 'L1_gnn_gate_logit': _L1_gnn_in['gate_logit'], 'L1_gnn_log_sigma': _L1_gnn_in['log_sigma']}

def reference(x, adj, L0_gnn_wq, L0_gnn_wk, L0_gnn_bm, L1_gnn_W_lang, L1_gnn_W_grav, L1_gnn_W_V, L1_gnn_W_O, L1_gnn_gate_logit, L1_gnn_log_sigma):
    import jax
    import jax.numpy as jnp

    def _L0_gnn_ref(x, wq, wk, wm, bm):
        import jax, jax.numpy as jnp
        import numpy as np
        NEG_SLOPE = 0.01
        q = jnp.einsum('c,bcn->bn', wq, x)
        k = jnp.einsum('c,bcn->bn', wk, x)
        scores = q[:, None, :] + k[:, :, None]
        scores = jnp.where(scores > 0, scores, NEG_SLOPE * scores)
        att = jax.nn.softmax(scores, axis=-1)
        agg = jnp.einsum('bcn,bmn->bcm', x, att)
        out = jnp.einsum('oc,bcm->bom', wm, agg) + bm[None, :, None]
        return jax.nn.relu(out)

    def _L1_gnn_ref(h, causal_mask, W_lang, W_grav, W_V, W_O, gate_logit, log_sigma):
        import jax, jax.numpy as jnp
        import numpy as np
        EPS = 1e-08

        def _row_stochastic_causal(A, causal_mask):
            A = A * causal_mask
            deg = jnp.maximum(A.sum(axis=-1, keepdims=True), EPS)
            return A / deg
        z_l = jnp.einsum('bnd,ed->bne', h, W_lang)
        z_g = jnp.einsum('bnd,ed->bne', h, W_grav)
        v = jnp.einsum('bnd,ed->bne', h, W_V)
        N = h.shape[-2]
        not_eye = 1.0 - jnp.eye(N, dtype=h.dtype)
        zn = z_l / jnp.maximum(jnp.linalg.norm(z_l, axis=-1, keepdims=True), EPS)
        A_l = jnp.maximum(jnp.einsum('bnd,bmd->bnm', zn, zn), 0.0) * not_eye
        sq = jnp.sum(z_g * z_g, axis=-1, keepdims=True)
        d2 = jnp.maximum(sq + jnp.swapaxes(sq, -1, -2) - 2.0 * jnp.einsum('bnd,bmd->bnm', z_g, z_g), 0.0)
        sigma = jnp.exp(log_sigma)
        A_g = jnp.exp(-d2 / (2.0 * sigma * sigma)) * not_eye
        K_l = _row_stochastic_causal(A_l, causal_mask)
        K_g = _row_stochastic_causal(A_g, causal_mask)
        w_l = jax.nn.sigmoid(gate_logit)
        K = w_l * K_l + (1.0 - w_l) * K_g
        out = jnp.einsum('bnm,bmd->bnd', K, v)
        return jnp.einsum('bnd,ed->bne', out, W_O)
    h = jnp.maximum(_layernorm(x, axis=-1), 0.0)
    x = x + _L0_gnn_ref(h, L0_gnn_wq, L0_gnn_wk, adj, L0_gnn_bm)
    h = jnp.maximum(_layernorm(x, axis=-1), 0.0)
    x = x + _L1_gnn_ref(h, adj, L1_gnn_W_lang, L1_gnn_W_grav, L1_gnn_W_V, L1_gnn_W_O, L1_gnn_gate_logit, L1_gnn_log_sigma)
    return x

_drawn_inputs = setup_inputs


def setup_inputs(seed=0):
    import zlib

    import numpy as np

    out = dict(_drawn_inputs(seed))
    spreads = {}
    factors = {'L0_gnn_wq': 8.0, 'L0_gnn_wk': 8.0, 'L0_gnn_bm': 6.6, 'L1_gnn_W_lang': 5.415}
    for name, (base, spread) in spreads.items():
        noise = np.random.default_rng([zlib.crc32(name.encode()), seed]).standard_normal(out[name].shape)
        drawn = base * np.exp(spread * noise) if base else spread * noise
        out[name] = jnp.asarray(drawn.astype(out[name].dtype))
    for name, factor in factors.items():
        out[name] = (out[name] * factor).astype(out[name].dtype)
    return out
```

```python
from collections import namedtuple
from contextlib import ExitStack

import concourse.bass as bass
from concourse import mybir

Batch = namedtuple("Batch", "n p half")


def after(b, k):
    return Batch(b.n + k, (b.p + k) % 2, b.half + (b.p + k) // 2)


def graph_layers_kernel(nc, x, adj, adj_wq_wk, bm, wl_t, wg_t, wv, wo_t, gate_logit, log_sigma, out):
    f32 = mybir.dt.float32
    f32r = mybir.dt.float32r
    ALU = mybir.AluOpType
    ACT = mybir.ActivationFunctionType
    AX_X = mybir.AxisListType.X

    B, C, N = x.shape
    P = 128
    RT = C // P
    FT = N // P
    CQ = C + 2
    LN_EPS = 1e-5
    DEG_EPS = 1e-8
    NORM_EPS = 1e-8
    SLOPE = 0.01
    SHIFT = 44.0
    T_MAX = 2 * SHIFT / (1 - SLOPE)

    x_v = x.rearrange("b (r p) n -> b p r n", p=P)
    out_v = out.rearrange("b (r p) n -> b p r n", p=P)

    ctx = ExitStack()
    with ctx:
        def sb(name, shape, dt=f32):
            return ctx.enter_context(nc.sbuf_tensor(name, shape, dt))

        def sem(name):
            return ctx.enter_context(nc.semaphore(name))

        ident = sb("ident", [P, P])
        ones_col = sb("ones_col", [P, 1])
        minus_half = sb("minus_half", [P, RT])
        neg_shift = sb("neg_shift", [P, 1])
        adj_off = sb("adj_off", [P, RT, C])
        bm_col = sb("bm_col", [P, RT])
        wcat = sb("wcat", [P, RT, CQ])
        wcat_hi = sb("wcat_hi", [P, RT, CQ], f32r)
        wcat_lo = sb("wcat_lo", [P, RT, CQ], f32r)
        stage_a = sb("stage_a", [P, FT, N])
        stage_b = sb("stage_b", [P, FT, N])
        wl_hi = sb("wl_hi", [P, FT, N], f32r)
        wl_lo = sb("wl_lo", [P, FT, N], f32r)
        wg_hi = sb("wg_hi", [P, FT, N], f32r)
        wg_lo = sb("wg_lo", [P, FT, N], f32r)
        m_hi = sb("m_hi", [P, FT, N], f32r)
        m_lo = sb("m_lo", [P, FT, N], f32r)
        gate_in = sb("gate_in", [P, 2])
        gate_exp = sb("gate_exp", [P, 2])
        gate_den = sb("gate_den", [P, 2])
        gate_inv = sb("gate_inv", [P, 2])
        xt = [sb(f"xt{p}", [P, RT, N]) for p in range(2)]
        x1 = [sb(f"x1_{p}", [P, RT, N]) for p in range(2)]
        stats = sb("stats", [P, 2, RT, 6])
        mean_var = sb("mean_var", [P, 2, RT, 2])
        var_eps = sb("var_eps", [P, 2, RT])
        rstd = sb("rstd", [P, 2, RT])
        shift = sb("shift", [P, 2, RT])
        h = sb("h", [P, RT, N])
        h_hi = sb("h_hi", [P, RT, N], f32r)
        h_lo = sb("h_lo", [P, RT, N], f32r)
        gt_hi = sb("gt_hi", [P, FT, C], f32r)
        gt_lo = sb("gt_lo", [P, FT, C], f32r)
        qk = sb("qk", [P, FT, 2])
        q_top = sb("q_top", [P, 1])
        q_max = sb("q_max", [P, 1])
        cols = sb("cols", [P, 2, FT])
        a_col = sb("a_col", [P, FT])
        b_col = sb("b_col", [P, FT])
        r_col = sb("r_col", [P, FT])
        r_row = sb("r_row", [P, N])
        pw = sb("pw", [P, FT, N])
        pw_hi = sb("pw_hi", [P, FT, N], f32r)
        pw_lo = sb("pw_lo", [P, FT, N], f32r)
        pair_sum = sb("pair_sum", [P, 2, N])
        pw_sum = sb("pw_sum", [P, N])
        rinv_col = sb("rinv_col", [P, FT])
        rinv_row = sb("rinv_row", [P, N])
        yn = sb("yn", [P, RT, N])
        h2 = sb("h2", [P, RT, N])
        h2t_hi = sb("h2t_hi", [P, FT, C], f32r)
        h2t_lo = sb("h2t_lo", [P, FT, C], f32r)
        zl_hi = sb("zl_hi", [P, FT, C], f32r)
        zl_lo = sb("zl_lo", [P, FT, C], f32r)
        zg_hi = sb("zg_hi", [P, FT, C], f32r)
        zg_lo = sb("zg_lo", [P, FT, C], f32r)
        v_hi = sb("v_hi", [P, RT, N], f32r)
        v_lo = sb("v_lo", [P, RT, N], f32r)
        diag = sb("diag", [P, 4, P])
        sq = sb("sq", [P, 2, RT])
        sq_guard = sb("sq_guard", [P, RT])
        rnorm = sb("rnorm", [P, RT])
        norm_row = sb("norm_row", [P, 2, C])
        al = sb("al", [P, RT, C])
        dist = sb("dist", [P, RT, C])
        ag = sb("ag", [P, RT, C])
        kl = sb("kl", [P, RT, C])
        kg = sb("kg", [P, RT, C])
        kmat = sb("kmat", [P, RT, C])
        row_sum = sb("row_sum", [P, 2, RT])
        deg_scale = sb("deg_scale", [P, 2, RT])
        gate_coef = sb("gate_coef", [P, 2, RT])
        deg = sb("deg", [P, 2, RT])
        deg_guard = sb("deg_guard", [P, 2, RT])
        deg_inv = sb("deg_inv", [P, 2, RT])
        row_coef = sb("row_coef", [P, 2, RT])
        kt_hi = sb("kt_hi", [P, RT, C], f32r)
        kt_lo = sb("kt_lo", [P, RT, C], f32r)

        bank = [ctx.enter_context(nc.psum_tensor(f"bank{i}", [P, 512], f32)) for i in range(8)]
        GT_BANK = [4, 2, 3, 4]
        M_BANK = [0, 1, 5, 6]
        SUM_BANK, ROW_BANK, GL_BANK, GG_BANK, KT_BANK = 4, 7, 5, 6, 4

        names = """weights_in adj_in small_in wlg_in wvo_in x_in0 x_in1 stored0 stored1
            ident_zero ident_done consts_done adj_off_done wcat_split gate_exp_done gate_den_done
            gate_inv_done gate_coef_done wlg_hi wlg_lo m_done m_hi_done m_lo_done
            stats1 aggr1 var1 rstd1 shift1 h_done h_hi_done h_lo_done
            gt_done gt_hi_done qk_done gt_lo_done q_top_done q_row_done q_max_done cols_done
            exps_done r_row_done r_copied pw_done pw_hi_done pw_lo_done pair_done sum_done
            y_done sums_done rinv_done rinv_row_done rinv_copied yn_done relu_done x1_done
            stats2 aggr2 var2 rstd2 shift2 h2_done h2t_done h2t_hi_done h2t_lo_done
            zl_done zl_hi_done zl_lo_done zg_done zg_hi_done zg_lo_done
            gl_done gg_done sq_done guard_done rnorm_done norm_row_done norm_copied
            al_done dist_done dist2_done ag_done kl_done kg_done scale_done deg_done
            deg_guard_done deg_inv_done row_coef_done kg_scaled_done k_done
            kt_done kt_hi_done kt_lo_done v_done v_hi_done v_lo_done out_done added""".split()
        s = namedtuple("Semaphores", names)(*[sem(n) for n in names])
        x_in = [s.x_in0, s.x_in1]
        stored = [s.stored0, s.stored1]

        block = ctx.enter_context(nc.Block())

        def f(t):
            return t.bitcast(f32)

        @block.sync
        def _(sp):
            def load_x(b):
                sp.dma_start(xt[b.p][:, :, :], x_v[b.n]).then_inc(x_in[b.p], 16)

            def load_next_x(b):
                sp.wait_ge(s.x1_done, RT * (b.n + 1))
                load_x(after(b, 2))

            def store(b):
                sp.wait_ge(s.added, RT * (b.n + 1))
                sp.dma_start(out_v[b.n], x1[b.p][:, :, :]).then_inc(stored[b.p], 16)

            load_x(Batch(0, 0, 0))
            sp.dma_start(wcat[:, :, :], adj_wq_wk.rearrange("(r p) o -> p r o", p=P)).then_inc(s.weights_in, 16)
            sp.dma_start(bm_col[:, :], bm.rearrange("(r p) -> p r", p=P),
                         allow_slow_non_contiguous=True).then_inc(s.small_in, 16)
            load_x(Batch(1, 1, 0))
            sp.dma_start(gate_in[:, 0:1], gate_logit.partition_broadcast(P)).then_inc(s.small_in, 16)
            sp.dma_start(gate_in[:, 1:2], log_sigma.partition_broadcast(P)).then_inc(s.small_in, 16)
            sp.dma_start(stage_a[:, :, :], wl_t.rearrange("(t p) e -> p t e", p=P)).then_inc(s.wlg_in, 16)
            sp.dma_start(stage_b[:, :, :], wg_t.rearrange("(t p) e -> p t e", p=P)).then_inc(s.wlg_in, 16)
            sp.dma_start(adj_off[:, :, :], adj.rearrange("(r p) m -> p r m", p=P)).then_inc(s.adj_in, 16)
            sp.wait_ge(s.wlg_lo, 2)
            sp.dma_start(stage_a[:, :, :], wv.rearrange("(t p) d -> p t d", p=P)).then_inc(s.wvo_in, 16)
            sp.dma_start(stage_b[:, :, :], wo_t.rearrange("(t p) e -> p t e", p=P)).then_inc(s.wvo_in, 16)
            load_next_x(Batch(0, 0, 0))
            with sp.Fori(0, (B - 4) // 2) as i:
                for k in (1, 2):
                    b = Batch(2 * i + k, k % 2, i + k // 2)
                    load_next_x(b)
                    store(after(b, -1))
            for n in range(B - 3, B):
                if n + 2 < B:
                    load_next_x(Batch(n, n % 2, n // 2))
                store(Batch(n - 1, (n - 1) % 2, (n - 1) // 2))
            store(Batch(B - 1, (B - 1) % 2, (B - 1) // 2))
            for p in range(2):
                sp.wait_ge(stored[p], 1 + 16 * (B // 2))

        def run_batches(eng, iteration):
            with eng.Fori(0, (B - 2) // 2) as i:
                for p in range(2):
                    iteration(Batch(2 * i + p, p, i), True, True)
            iteration(Batch(B - 2, 0, B // 2 - 1), True, False)
            iteration(Batch(B - 1, 1, B // 2 - 1), False, False)

        FIRST = Batch(0, 0, 0)

        @block.tensor
        def _(pe):
            def product(dst, pairs):
                last = None
                for n, (lh, ll, rh, rl) in enumerate(pairs):
                    nc.tensor.matmul(dst, lh, rh, start=(n == 0), stop=False)
                    nc.tensor.matmul(dst, lh, rl, start=False, stop=False)
                    last = nc.tensor.matmul(dst, ll, rh, start=False, stop=(n == len(pairs) - 1))
                return last

            def row_of(dst, col):
                return nc.tensor.matmul(dst, col.broadcast_to((P, P)), ident[:, :], is_transpose=True,
                                        start=True, stop=True)

            def adj_h(c):
                pe.wait_ge(s.h_hi_done, c.n + 1)
                pe.wait_ge(s.h_lo_done, c.n + 1)
                for j in range(FT):
                    if j == FT - 1:
                        pe.wait_ge(s.gt_lo_done, FT * c.n + 1)
                    js = slice(j * P, (j + 1) * P)
                    product(bank[GT_BANK[j]][:, 0:CQ],
                            [(h_hi[:, r, js], h_lo[:, r, js], wcat_hi[:, r, :], wcat_lo[:, r, :])
                             for r in range(RT)]).then_inc(s.gt_done, 1)

            def max_q(c):
                pe.wait_ge(s.q_top_done, c.n + 1)
                row_of(bank[ROW_BANK][:, 0:P], q_top[:, 0:1]).then_inc(s.q_row_done, 1)

            def rows_r(c):
                pe.wait_ge(s.exps_done, 3 * (c.n + 1))
                for j in range(FT):
                    last = row_of(bank[ROW_BANK][:, j * P:(j + 1) * P], r_col[:, j:j + 1])
                last.then_inc(s.r_row_done, 1)

            def weighted(c, r):
                for j in range(FT):
                    if r == 0:
                        pe.wait_ge(s.pw_hi_done, FT * c.n + j + 1)
                        pe.wait_ge(s.pw_lo_done, FT * c.n + j + 1)
                        if j == 0:
                            pe.wait_ge(s.gt_lo_done, FT * (c.n + 1))
                    rs = slice(r * P, (r + 1) * P)
                    dst = bank[2 + r][:, :]
                    nc.tensor.matmul(dst, gt_hi[:, j, rs], pw_hi[:, j, :], start=(j == 0), stop=False)
                    nc.tensor.matmul(dst, gt_hi[:, j, rs], pw_lo[:, j, :], start=False, stop=False)
                    last = nc.tensor.matmul(dst, gt_lo[:, j, rs], pw_hi[:, j, :], start=False, stop=(j == FT - 1))
                last.then_inc(s.y_done, 1)

            def column_sums(c):
                pe.wait_ge(s.sum_done, c.n + 1)
                for j in range(FT):
                    last = nc.tensor.matmul(bank[SUM_BANK][:, j:j + 1], pw_sum[:, j * P:(j + 1) * P],
                                            ones_col[:, :], start=True, stop=True)
                last.then_inc(s.sums_done, 1)

            def rows_rinv(c, norms_before):
                pe.wait_ge(s.rinv_done, c.n + 1)
                pe.wait_ge(s.r_copied, c.n + 1)
                if norms_before:
                    pe.wait_ge(s.norm_copied, c.n)
                for j in range(FT):
                    last = row_of(bank[ROW_BANK][:, j * P:(j + 1) * P], rinv_col[:, j:j + 1])
                last.then_inc(s.rinv_row_done, 1)

            def transpose_h2(c):
                pe.wait_ge(s.h2_done, RT * (c.n + 1))
                for half in range(2):
                    for t in range(2):
                        for r in range(RT):
                            d = 2 * half + t
                            last = nc.tensor.transpose(bank[2 + half][:, t * C + r * P:t * C + (r + 1) * P],
                                                       h2[:, r, d * P:(d + 1) * P], ident[:, :])
                    last.then_inc(s.h2t_done, 1)

            def project(b, w_hi, w_lo, done, tiles):
                for e in tiles:
                    es = slice(e * P, (e + 1) * P)
                    last = product(bank[e // 2][:, (e % 2) * C:(e % 2 + 1) * C],
                                   [(w_hi[:, d, es], w_lo[:, d, es], h2t_hi[:, d, :], h2t_lo[:, d, :])
                                    for d in range(FT)])
                last.then_inc(done, 1)

            def gram(b, z_hi, z_lo, where, done):
                for r in range(RT):
                    rs = slice(r * P, (r + 1) * P)
                    last = product(bank[where][:, r * C:(r + 1) * C],
                                   [(z_hi[:, e, rs], z_lo[:, e, rs], z_hi[:, e, :], z_lo[:, e, :])
                                    for e in range(FT)])
                last.then_inc(done, 1)

            def rows_norms(b):
                pe.wait_ge(s.rnorm_done, b.n + 1)
                pe.wait_ge(s.sq_done, 4 * (b.n + 1))
                for r in range(RT):
                    row_of(bank[ROW_BANK][:, r * P:(r + 1) * P], rnorm[:, r:r + 1])
                for r in range(RT):
                    last = row_of(bank[ROW_BANK][:, C + r * P:C + (r + 1) * P], sq[:, 1, r:r + 1])
                last.then_inc(s.norm_row_done, 1)

            def values(b, r):
                rs = slice(r * P, (r + 1) * P)
                product(bank[r][:, :], [(h2t_hi[:, d, rs], h2t_lo[:, d, rs], m_hi[:, d, :], m_lo[:, d, :])
                                        for d in range(FT)]).then_inc(s.v_done, 1)

            def transpose_k(b):
                pe.wait_ge(s.k_done, RT * (b.n + 1))
                for m in range(RT):
                    for r in range(RT):
                        last = nc.tensor.transpose(bank[KT_BANK][:, m * C + r * P:m * C + (r + 1) * P],
                                                   kmat[:, r, m * P:(m + 1) * P], ident[:, :])
                last.then_inc(s.kt_done, 1)

            def mix(b):
                pe.wait_ge(s.kt_lo_done, b.n + 1)
                pe.wait_ge(s.v_lo_done, RT * (b.n + 1))
                for r in range(RT):
                    rs = slice(r * P, (r + 1) * P)
                    product(bank[GL_BANK + r][:, :],
                            [(kt_hi[:, m, rs], kt_lo[:, m, rs], v_hi[:, m, :], v_lo[:, m, :])
                             for m in range(RT)]).then_inc(s.out_done, 1)

            pe.wait_ge(s.ident_done, 1)
            pe.wait_ge(s.consts_done, 2)
            pe.wait_ge(s.wcat_split, 2)
            adj_h(FIRST)
            max_q(FIRST)
            rows_r(FIRST)
            pe.wait_ge(s.wvo_in, 32)
            for d in range(FT):
                for k in range(FT):
                    last = nc.tensor.matmul(bank[M_BANK[d]][:, :], stage_a[:, k, d * P:(d + 1) * P],
                                            stage_b[:, k, :], start=(k == 0), stop=(k == FT - 1))
                last.then_inc(s.m_done, 1)
            weighted(FIRST, 0)
            column_sums(FIRST)
            weighted(FIRST, 1)
            rows_rinv(FIRST, False)
            pe.wait_ge(s.m_lo_done, FT)
            transpose_h2(FIRST)

            def iteration(b, layer0, _):
                c = after(b, 1)
                pe.wait_ge(s.h2t_hi_done, 2 * (b.n + 1))
                pe.wait_ge(s.h2t_lo_done, 2 * (b.n + 1))
                project(b, wl_hi, wl_lo, s.zl_done, (0, 1))
                project(b, wl_hi, wl_lo, s.zl_done, (2, 3))
                if layer0:
                    adj_h(c)
                pe.wait_ge(s.zl_lo_done, 2 * b.n + 1)
                project(b, wg_hi, wg_lo, s.zg_done, (0, 1))
                if layer0:
                    max_q(c)
                pe.wait_ge(s.zl_lo_done, 2 * b.n + 2)
                project(b, wg_hi, wg_lo, s.zg_done, (2, 3))
                if layer0:
                    rows_r(c)
                gram(b, zl_hi, zl_lo, GL_BANK, s.gl_done)
                pe.wait_ge(s.zg_lo_done, 2 * (b.n + 1))
                gram(b, zg_hi, zg_lo, GG_BANK, s.gg_done)
                if layer0:
                    weighted(c, 0)
                    column_sums(c)
                rows_norms(b)
                if layer0:
                    weighted(c, 1)
                    rows_rinv(c, True)
                values(b, 0)
                transpose_k(b)
                values(b, 1)
                if layer0:
                    transpose_h2(c)
                mix(b)

            run_batches(pe, iteration)

        @block.scalar
        def _(act):
            def normalised(b, src, done, which, ready):
                act.wait_ge(ready, b.n + 1)
                for r in range(RT):
                    nc.scalar.activation(done[0][:, r, :], src[:, r, :], ACT.Relu,
                                         bias=shift[:, which, r:r + 1],
                                         scale=rstd[:, which, r:r + 1]).then_inc(done[1], 1)

            def high_h(a):
                act.wait_ge(s.h_done, RT * (a.n + 1))
                nc.scalar.copy(h_hi[:, :, :], h[:, :, :]).then_inc(s.h_hi_done, 1)

            def high_gt(c):
                for j in range(FT):
                    act.wait_ge(s.gt_done, FT * c.n + j + 1)
                    nc.scalar.copy(gt_hi[:, j, :], bank[GT_BANK[j]][:, 0:C]).then_inc(s.gt_hi_done, 1)

            def exps(c):
                act.wait_ge(s.cols_done, 2 * (c.n + 1))
                nc.scalar.activation(r_col[:, :], cols[:, 1, :], ACT.Exp, bias=neg_shift[:, 0:1],
                                     scale=1 - SLOPE).then_inc(s.exps_done, 1)
                nc.scalar.activation(a_col[:, :], cols[:, 0, :], ACT.Exp).then_inc(s.exps_done, 1)
                nc.scalar.activation(b_col[:, :], cols[:, 0, :], ACT.Exp, bias=neg_shift[:, 0:1],
                                     scale=SLOPE).then_inc(s.exps_done, 1)

            def copy_r(c):
                act.wait_ge(s.r_row_done, c.n + 1)
                nc.scalar.copy(r_row[:, :], bank[ROW_BANK][:, :]).then_inc(s.r_copied, 1)

            def high_pw(c):
                for j in range(FT):
                    act.wait_ge(s.pw_done, FT * c.n + j + 1)
                    nc.scalar.copy(pw_hi[:, j, :], pw[:, j, :]).then_inc(s.pw_hi_done, 1)

            def copy_rinv(c):
                act.wait_ge(s.rinv_row_done, c.n + 1)
                nc.scalar.copy(rinv_row[:, :], bank[ROW_BANK][:, :]).then_inc(s.rinv_copied, 1)

            def relu_y(c):
                for r in range(RT):
                    act.wait_ge(s.yn_done, RT * c.n + r + 1)
                    nc.scalar.activation(yn[:, r, :], yn[:, r, :], ACT.Relu,
                                         bias=bm_col[:, r:r + 1]).then_inc(s.relu_done, 1)

            def high(wait_on, count, dst, src, done):
                act.wait_ge(wait_on, count)
                nc.scalar.copy(dst, src).then_inc(done, 1)

            def two_tiles(t, i):
                return t[:, 2 * i:2 * i + 2, :].rearrange("p t c -> p (t c)")

            def high_h2t(c):
                for i in range(2):
                    high(s.h2t_done, 2 * c.n + i + 1, two_tiles(h2t_hi, i), bank[2 + i][:, :], s.h2t_hi_done)

            act.wait_ge(s.consts_done, 2)
            act.wait_ge(s.weights_in, 16)
            nc.scalar.copy(wcat_hi[:, :, :], wcat[:, :, :]).then_inc(s.wcat_split, 1)
            normalised(FIRST, xt[0], (h, s.h_done), 0, s.shift1)
            high_h(FIRST)
            act.wait_ge(s.small_in, 48)
            nc.scalar.activation(gate_exp[:, 0:1], gate_in[:, 0:1], ACT.Exp, scale=-1.0).then_inc(s.gate_exp_done, 1)
            nc.scalar.activation(gate_exp[:, 1:2], gate_in[:, 1:2], ACT.Exp).then_inc(s.gate_exp_done, 1)
            high_gt(FIRST)
            exps(FIRST)
            copy_r(FIRST)
            act.wait_ge(s.wlg_in, 32)
            nc.scalar.copy(wl_hi[:, :, :], stage_a[:, :, :]).then_inc(s.wlg_hi, 1)
            nc.scalar.copy(wg_hi[:, :, :], stage_b[:, :, :]).then_inc(s.wlg_hi, 1)
            high_pw(FIRST)
            act.wait_ge(s.h_lo_done, 1)
            act.wait_ge(s.gt_done, FT)
            normalised(after(FIRST, 1), xt[1], (h, s.h_done), 0, s.shift1)
            high_h(after(FIRST, 1))
            for d in range(FT):
                high(s.m_done, d + 1, m_hi[:, d, :], bank[M_BANK[d]][:, :], s.m_hi_done)
            copy_rinv(FIRST)
            relu_y(FIRST)
            normalised(FIRST, x1[0], (h2, s.h2_done), 1, s.shift2)
            high_h2t(FIRST)

            def iteration(b, layer0, norm0):
                c, a = after(b, 1), after(b, 2)
                high(s.zl_done, 2 * b.n + 1, two_tiles(zl_hi, 0), bank[0][:, :], s.zl_hi_done)
                high(s.zl_done, 2 * b.n + 2, two_tiles(zl_hi, 1), bank[1][:, :], s.zl_hi_done)
                if layer0:
                    high_gt(c)
                if norm0:
                    normalised(a, xt[a.p], (h, s.h_done), 0, s.shift1)
                    high_h(a)
                high(s.zg_done, 2 * b.n + 1, two_tiles(zg_hi, 0), bank[0][:, :], s.zg_hi_done)
                if layer0:
                    exps(c)
                high(s.zg_done, 2 * b.n + 2, two_tiles(zg_hi, 1), bank[1][:, :], s.zg_hi_done)
                if layer0:
                    copy_r(c)
                    high_pw(c)
                high(s.norm_row_done, b.n + 1, norm_row[:, :, :].rearrange("p s c -> p (s c)"),
                     bank[ROW_BANK][:, :], s.norm_copied)
                if layer0:
                    copy_rinv(c)
                act.wait_ge(s.dist2_done, RT * (b.n + 1))
                nc.scalar.activation(ag[:, :, :], dist[:, :, :], ACT.Exp,
                                     scale=gate_inv[:, 1:2]).then_inc(s.ag_done, 1)
                if layer0:
                    relu_y(c)
                high(s.v_done, RT * b.n + 1, v_hi[:, 0, :], bank[0][:, :], s.v_hi_done)
                if layer0:
                    normalised(c, x1[c.p], (h2, s.h2_done), 1, s.shift2)
                high(s.kt_done, b.n + 1, kt_hi[:, :, :].rearrange("p r c -> p (r c)"), bank[KT_BANK][:, :],
                     s.kt_hi_done)
                high(s.v_done, RT * b.n + 2, v_hi[:, 1, :], bank[1][:, :], s.v_hi_done)
                if layer0:
                    high_h2t(c)

            run_batches(act, iteration)

        @block.gpsimd
        def _(pool):
            def power(dst, src, ready, count, done):
                pool.wait_ge(ready, count)
                nc.gpsimd.tensor_tensor(dst, src, minus_half[:, :], ALU.pow).then_inc(done, 1)

            def sum_pw(c):
                pool.wait_ge(s.pw_done, FT * (c.n + 1))
                nc.gpsimd.tensor_tensor(pair_sum[:, :, :], pw[:, 0:2, :], pw[:, 2:4, :], ALU.add).then_inc(s.pair_done, 1)
                pool.wait_ge(s.pair_done, c.n + 1)
                nc.gpsimd.tensor_tensor(pw_sum[:, :], pair_sum[:, 0, :], pair_sum[:, 1, :], ALU.add).then_inc(s.sum_done, 1)

            def residual(c, stored_before):
                if stored_before is not None:
                    pool.wait_ge(stored[c.p], stored_before)
                for r in range(RT):
                    pool.wait_ge(s.relu_done, RT * c.n + r + 1)
                    nc.gpsimd.tensor_tensor(x1[c.p][:, r, :], xt[c.p][:, r, :], yn[:, r, :], ALU.add).then_inc(s.x1_done, 1)

            nc.gpsimd.memset(minus_half[:, :], -0.5).then_inc(s.consts_done, 1)
            nc.gpsimd.memset(ident[:, :], 0.0).then_inc(s.ident_zero, 1)
            pool.wait_ge(s.ident_zero, 1)
            nc.gpsimd.affine_select(out=ident[:, :], in_=ident[:, :], compare_op=ALU.not_equal, fill=1.0, base=0,
                                    pattern=[[-1, P]], channel_multiplier=1).then_inc(s.ident_done, 1)
            pool.wait_ge(s.consts_done, 2)
            power(rstd[:, 0, :], var_eps[:, 0, :], s.var1, 1, s.rstd1)
            pool.wait_ge(s.adj_in, 16)
            nc.gpsimd.affine_select(out=adj_off[:, :, :], in_=adj_off[:, :, :], compare_op=ALU.not_equal, fill=0.0,
                                    base=0, pattern=[[P, RT], [-1, C]], channel_multiplier=1).then_inc(s.adj_off_done, 1)
            power(rstd[:, 0, :], var_eps[:, 0, :], s.var1, 2, s.rstd1)
            sum_pw(FIRST)
            residual(FIRST, None)
            power(rstd[:, 1, :], var_eps[:, 1, :], s.var2, 1, s.rstd2)

            def iteration(b, layer0, norm0):
                c, a = after(b, 1), after(b, 2)
                if norm0:
                    power(rstd[:, 0, :], var_eps[:, 0, :], s.var1, a.n + 1, s.rstd1)
                if layer0:
                    sum_pw(c)
                power(rnorm[:, :], sq_guard[:, :], s.guard_done, b.n + 1, s.rnorm_done)
                if layer0:
                    residual(c, 1 + 16 * c.half)
                    power(rstd[:, 1, :], var_eps[:, 1, :], s.var2, c.n + 1, s.rstd2)

            run_batches(pool, iteration)

        @block.vector
        def _(dve):
            def low(wait_on, count, dst, src, hi, done):
                dve.wait_ge(wait_on, count)
                nc.vector.tensor_tensor(dst, src, f(hi), ALU.subtract).then_inc(done, 1)

            def statistics(b, src, which, src_ready, counts, stat_sem):
                for r in range(RT):
                    dve.wait_ge(src_ready, counts[r])
                    nc.vector.bn_stats(stats[:, which, r, :], src[:, r, :]).then_inc(stat_sem, 1)
                dve.wait_ge(stat_sem, RT * (b.n + 1))

            def aggregate(b, which, aggr_sem, var_sem):
                for r in range(RT):
                    nc.vector.bn_aggr(mean_var[:, which, r, :], stats[:, which, r, :]).then_inc(aggr_sem, 1)
                dve.wait_ge(aggr_sem, RT * (b.n + 1))
                nc.vector.tensor_scalar(var_eps[:, which, :], mean_var[:, which, :, 1], LN_EPS, None,
                                        ALU.add).then_inc(var_sem, 1)

            def statistics1(a):
                statistics(a, xt[a.p], 0, x_in[a.p], [16 * (a.half + 1)] * RT, s.stats1)

            def aggregate1(a):
                aggregate(a, 0, s.aggr1, s.var1)

            def statistics2(c):
                statistics(c, x1[c.p], 1, s.x1_done, [RT * c.n + r + 1 for r in range(RT)], s.stats2)

            def aggregate2(c):
                aggregate(c, 1, s.aggr2, s.var2)

            def minus_mean_rstd(b, which, rstd_sem, shift_sem):
                dve.wait_ge(rstd_sem, b.n + 1)
                nc.vector.scalar_tensor_tensor(out=shift[:, which, :], in0=mean_var[:, which, :, 0], scalar=-1.0,
                                               in1=rstd[:, which, :], op0=ALU.mult, op1=ALU.mult).then_inc(shift_sem, 1)

            def low_gt(c):
                for j in range(FT):
                    dve.wait_ge(s.gt_hi_done, FT * c.n + j + 1)
                    nc.vector.tensor_copy(qk[:, j, :], bank[GT_BANK[j]][:, C:CQ]).then_inc(s.qk_done, 1)
                    nc.vector.tensor_tensor(gt_lo[:, j, :], bank[GT_BANK[j]][:, 0:C], f(gt_hi[:, j, :]),
                                            ALU.subtract).then_inc(s.gt_lo_done, 1)
                dve.wait_ge(s.qk_done, FT * (c.n + 1))
                nc.vector.reduce_max(q_top[:, :], qk[:, :, 0], AX_X).then_inc(s.q_top_done, 1)

            def columns(c):
                dve.wait_ge(s.q_row_done, c.n + 1)
                nc.vector.reduce_max(q_max[:, :], bank[ROW_BANK][:, 0:P], AX_X).then_inc(s.q_max_done, 1)
                dve.wait_ge(s.q_max_done, c.n + 1)
                nc.vector.tensor_scalar(cols[:, 1, :], qk[:, :, 1], q_max[:, 0:1], T_MAX, ALU.add,
                                        ALU.min).then_inc(s.cols_done, 1)
                nc.vector.tensor_scalar(cols[:, 0, :], qk[:, :, 0], q_max[:, 0:1], None,
                                        ALU.subtract).then_inc(s.cols_done, 1)

            def weights_p(c):
                dve.wait_ge(s.r_copied, c.n + 1)
                dve.wait_ge(s.exps_done, 3 * (c.n + 1))
                for j in range(FT):
                    nc.vector.tensor_scalar(pw[:, j, :], r_row[:, :], a_col[:, j:j + 1], b_col[:, j:j + 1],
                                            ALU.mult, ALU.max).then_inc(s.pw_done, 1)

            def low_p(c):
                for j in range(FT):
                    low(s.pw_hi_done, FT * c.n + j + 1, pw_lo[:, j, :], pw[:, j, :], pw_hi[:, j, :], s.pw_lo_done)

            def invert_sums(c):
                dve.wait_ge(s.sums_done, c.n + 1)
                nc.vector.reciprocal(rinv_col[:, :], bank[SUM_BANK][:, 0:FT]).then_inc(s.rinv_done, 1)

            def normalise_y(c):
                dve.wait_ge(s.rinv_copied, c.n + 1)
                for r in range(RT):
                    dve.wait_ge(s.y_done, RT * c.n + r + 1)
                    nc.vector.tensor_tensor(yn[:, r, :], bank[2 + r][:, :], rinv_row[:, :], ALU.mult).then_inc(s.yn_done, 1)

            def two_tiles(t, i):
                return t[:, 2 * i:2 * i + 2, :].rearrange("p t c -> p (t c)")

            def low_h2t(c):
                for i in range(2):
                    low(s.h2t_hi_done, 2 * c.n + i + 1, two_tiles(h2t_lo, i), bank[2 + i][:, :],
                        two_tiles(h2t_hi, i), s.h2t_lo_done)

            def squared_norms(b):
                for g, (where, ready) in enumerate(((GL_BANK, s.gl_done), (GG_BANK, s.gg_done))):
                    dve.wait_ge(ready, b.n + 1)
                    for r in range(RT):
                        at = r * C + r * P
                        nc.vector.tensor_tensor_reduce(
                            out=diag[:, 2 * g + r, :], in0=bank[where][:, at:at + P], in1=ident[:, :], scale=1.0,
                            scalar=0.0, op0=ALU.mult, op1=ALU.add, accum_out=sq[:, g, r:r + 1]).then_inc(s.sq_done, 1)
                    if g == 0:
                        dve.wait_ge(s.sq_done, 4 * b.n + RT)
                        nc.vector.tensor_scalar(sq_guard[:, :], sq[:, 0, :], NORM_EPS * NORM_EPS, None,
                                                ALU.max).then_inc(s.guard_done, 1)

            def kernels(b):
                dve.wait_ge(s.norm_copied, b.n + 1)
                dve.wait_ge(s.sq_done, 4 * (b.n + 1))
                gg = bank[GG_BANK][:, :].rearrange("p (r c) -> p r c", r=RT)
                gl = bank[GL_BANK][:, :].rearrange("p (r c) -> p r c", r=RT)
                nc.vector.scalar_tensor_tensor(
                    out=dist[:, :, :], in0=gg, scalar=-2.0, in1=norm_row[:, 1:2, :].broadcast_to((P, RT, C)),
                    op0=ALU.mult, op1=ALU.add).then_inc(s.dist_done, 1)
                nc.vector.scalar_tensor_tensor(
                    out=al[:, :, :], in0=gl, scalar=0.0, in1=norm_row[:, 0:1, :].broadcast_to((P, RT, C)),
                    op0=ALU.max, op1=ALU.mult).then_inc(s.al_done, 1)
                dve.wait_ge(s.dist_done, b.n + 1)
                for r in range(RT):
                    nc.vector.tensor_scalar(dist[:, r, :], dist[:, r, :], sq[:, 1, r:r + 1], 0.0, ALU.add,
                                            ALU.max).then_inc(s.dist2_done, 1)

            def masked(b, src, ready, count, dst, g, done):
                dve.wait_ge(ready, count)
                for r in range(RT):
                    nc.vector.tensor_tensor_reduce(
                        out=dst[:, r, :], in0=src[:, r, :], in1=adj_off[:, r, :], scale=1.0, scalar=0.0,
                        op0=ALU.mult, op1=ALU.add, accum_out=row_sum[:, g, r:r + 1]).then_inc(done, 1)

            def row_scales(b):
                nc.vector.tensor_copy(deg_scale[:, 0, :], rnorm[:, :]).then_inc(s.scale_done, 1)
                nc.vector.tensor_scalar(gate_coef[:, 0, :], rnorm[:, :], gate_inv[:, 0:1], None,
                                        ALU.mult).then_inc(s.scale_done, 1)

            def combine(b):
                dve.wait_ge(s.kl_done, RT * (b.n + 1))
                dve.wait_ge(s.kg_done, RT * (b.n + 1))
                dve.wait_ge(s.scale_done, 2 * (b.n + 1))
                nc.vector.tensor_tensor(deg[:, :, :], row_sum[:, :, :], deg_scale[:, :, :], ALU.mult).then_inc(s.deg_done, 1)
                dve.wait_ge(s.deg_done, b.n + 1)
                nc.vector.tensor_scalar(deg_guard[:, :, :], deg[:, :, :], DEG_EPS, None, ALU.max).then_inc(s.deg_guard_done, 1)
                dve.wait_ge(s.deg_guard_done, b.n + 1)
                nc.vector.reciprocal(deg_inv[:, :, :], deg_guard[:, :, :]).then_inc(s.deg_inv_done, 1)
                dve.wait_ge(s.deg_inv_done, b.n + 1)
                nc.vector.tensor_tensor(row_coef[:, :, :], deg_inv[:, :, :], gate_coef[:, :, :], ALU.mult).then_inc(s.row_coef_done, 1)
                dve.wait_ge(s.row_coef_done, b.n + 1)
                for r in range(RT):
                    nc.vector.tensor_scalar(dist[:, r, :], kg[:, r, :], row_coef[:, 1, r:r + 1], None,
                                            ALU.mult).then_inc(s.kg_scaled_done, 1)
                for r in range(RT):
                    dve.wait_ge(s.kg_scaled_done, RT * b.n + r + 1)
                    nc.vector.scalar_tensor_tensor(
                        out=kmat[:, r, :], in0=kl[:, r, :], scalar=row_coef[:, 0, r:r + 1], in1=dist[:, r, :],
                        op0=ALU.mult, op1=ALU.add).then_inc(s.k_done, 1)

            def low_v(b, r):
                low(s.v_hi_done, RT * b.n + r + 1, v_lo[:, r, :], bank[r][:, :], v_hi[:, r, :], s.v_lo_done)

            def low_kt(b):
                low(s.kt_hi_done, b.n + 1, kt_lo[:, :, :].rearrange("p r c -> p (r c)"), bank[KT_BANK][:, :],
                    kt_hi[:, :, :].rearrange("p r c -> p (r c)"), s.kt_lo_done)

            def add_result(b):
                for r in range(RT):
                    dve.wait_ge(s.out_done, RT * b.n + r + 1)
                    nc.vector.tensor_tensor(x1[b.p][:, r, :], bank[GL_BANK + r][:, :], x1[b.p][:, r, :],
                                            ALU.add).then_inc(s.added, 1)

            nc.vector.memset(neg_shift[:, :], -SHIFT).then_inc(stored[0], 1)
            nc.vector.memset(deg_scale[:, 1, :], 1.0).then_inc(stored[1], 1)
            nc.vector.memset(ones_col[:, :], 1.0).then_inc(s.consts_done, 1)
            dve.wait_ge(s.consts_done, 2)
            statistics1(FIRST)
            aggregate1(FIRST)
            low(s.wcat_split, 1, wcat_lo[:, :, :], wcat[:, :, :], wcat_hi[:, :, :], s.wcat_split)
            minus_mean_rstd(FIRST, 0, s.rstd1, s.shift1)
            low(s.h_hi_done, 1, h_lo[:, :, :], h[:, :, :], h_hi[:, :, :], s.h_lo_done)
            dve.wait_ge(s.gate_exp_done, 2)
            nc.vector.tensor_scalar(gate_den[:, 0:1], gate_exp[:, 0:1], 1.0, None, ALU.add).then_inc(s.gate_den_done, 1)
            nc.vector.tensor_scalar(gate_den[:, 1:2], gate_exp[:, 1:2], gate_exp[:, 1:2], -2.0, ALU.mult,
                                    ALU.mult).then_inc(s.gate_den_done, 1)
            dve.wait_ge(s.gate_den_done, 2)
            nc.vector.reciprocal(gate_inv[:, :], gate_den[:, :]).then_inc(s.gate_inv_done, 1)
            dve.wait_ge(s.gate_inv_done, 1)
            for r in range(RT):
                nc.vector.tensor_scalar(gate_coef[:, 1, r:r + 1], gate_inv[:, 0:1], -1.0, 1.0, ALU.mult,
                                        ALU.add).then_inc(s.gate_coef_done, 1)
            low_gt(FIRST)
            columns(FIRST)
            low(s.wlg_hi, 1, wl_lo[:, :, :], stage_a[:, :, :], wl_hi[:, :, :], s.wlg_lo)
            low(s.wlg_hi, 2, wg_lo[:, :, :], stage_b[:, :, :], wg_hi[:, :, :], s.wlg_lo)
            weights_p(FIRST)
            low_p(FIRST)
            statistics1(after(FIRST, 1))
            aggregate1(after(FIRST, 1))
            minus_mean_rstd(after(FIRST, 1), 0, s.rstd1, s.shift1)
            low(s.h_hi_done, 2, h_lo[:, :, :], h[:, :, :], h_hi[:, :, :], s.h_lo_done)
            for d in range(FT):
                low(s.m_hi_done, d + 1, m_lo[:, d, :], bank[M_BANK[d]][:, :], m_hi[:, d, :], s.m_lo_done)
            invert_sums(FIRST)
            normalise_y(FIRST)
            statistics2(FIRST)
            aggregate2(FIRST)
            minus_mean_rstd(FIRST, 1, s.rstd2, s.shift2)
            low_h2t(FIRST)
            dve.wait_ge(s.adj_off_done, 1)
            dve.wait_ge(s.gate_coef_done, 2)

            def iteration(b, layer0, norm0):
                c, a = after(b, 1), after(b, 2)
                if norm0:
                    statistics1(a)
                low(s.zl_hi_done, 2 * b.n + 1, two_tiles(zl_lo, 0), bank[0][:, :], two_tiles(zl_hi, 0), s.zl_lo_done)
                if norm0:
                    aggregate1(a)
                    minus_mean_rstd(a, 0, s.rstd1, s.shift1)
                low(s.zl_hi_done, 2 * b.n + 2, two_tiles(zl_lo, 1), bank[1][:, :], two_tiles(zl_hi, 1), s.zl_lo_done)
                if layer0:
                    low_gt(c)
                if norm0:
                    low(s.h_hi_done, a.n + 1, h_lo[:, :, :], h[:, :, :], h_hi[:, :, :], s.h_lo_done)
                low(s.zg_hi_done, 2 * b.n + 1, two_tiles(zg_lo, 0), bank[0][:, :], two_tiles(zg_hi, 0), s.zg_lo_done)
                if layer0:
                    columns(c)
                low(s.zg_hi_done, 2 * b.n + 2, two_tiles(zg_lo, 1), bank[1][:, :], two_tiles(zg_hi, 1), s.zg_lo_done)
                if layer0:
                    weights_p(c)
                    low_p(c)
                squared_norms(b)
                if layer0:
                    invert_sums(c)
                kernels(b)
                if layer0:
                    normalise_y(c)
                masked(b, al, s.al_done, b.n + 1, kl, 0, s.kl_done)
                masked(b, ag, s.ag_done, b.n + 1, kg, 1, s.kg_done)
                if layer0:
                    statistics2(c)
                row_scales(b)
                if layer0:
                    aggregate2(c)
                combine(b)
                if layer0:
                    minus_mean_rstd(c, 1, s.rstd2, s.shift2)
                low_v(b, 0)
                low_kt(b)
                low_v(b, 1)
                if layer0:
                    low_h2t(c)
                add_result(b)

            run_batches(dve, iteration)


def kernel(**inputs):
    import numpy as np
    import concourse.bacc as bacc
    from concourse import mybir as mb
    from concourse.bass_utils import run_bass_kernel_spmd

    given = {name: np.asarray(a) for name, a in inputs.items()}
    laid = {
        "x": given["x"],
        "adj": given["adj"],
        "adj_wq_wk": np.concatenate([given["adj"].T, given["L0_gnn_wq"][:, None], given["L0_gnn_wk"][:, None]], axis=1),
        "bm": given["L0_gnn_bm"],
        "wl_t": given["L1_gnn_W_lang"].T,
        "wg_t": given["L1_gnn_W_grav"].T,
        "wv": given["L1_gnn_W_V"],
        "wo_t": given["L1_gnn_W_O"].T,
        "gate_logit": given["L1_gnn_gate_logit"].reshape(1),
        "log_sigma": given["L1_gnn_log_sigma"].reshape(1),
    }
    nc = bacc.Bacc("TRN2", target_bir_lowering=False, num_devices=1)
    arrays, args = {}, []
    for name, a in laid.items():
        arrays[f"in_{name}"] = np.ascontiguousarray(a)
        args.append(nc.dram_tensor(f"in_{name}", a.shape, mb.dt.from_np(a.dtype), kind="ExternalInput").ap())
    args.append(nc.dram_tensor("out_x", given["x"].shape, mb.dt.float32, kind="ExternalOutput").ap())
    graph_layers_kernel(nc, *args)
    r = run_bass_kernel_spmd(nc, [arrays], core_ids=[0])
    return r.results[0]["out_x"]
```

```python
from collections import namedtuple
from contextlib import ExitStack

import concourse.bass as bass
from concourse import mybir

Batch = namedtuple("Batch", "n p half")


def after(b, k):
    return Batch(b.n + k, (b.p + k) % 2, b.half + (b.p + k) // 2)


def graph_layers_kernel(nc, x, adj, adj_wq_wk, bm, wl_t, wg_t, wv, wo_t, gate_logit, log_sigma, out):
    f32 = mybir.dt.float32
    f32r = mybir.dt.float32r
    ALU = mybir.AluOpType
    ACT = mybir.ActivationFunctionType
    AX_X = mybir.AxisListType.X

    B, C, N = x.shape
    P = 128
    RT = C // P
    FT = N // P
    CQ = C + 2
    LN_EPS = 1e-5
    DEG_EPS = 1e-8
    NORM_EPS = 1e-8
    SLOPE = 0.01
    SHIFT = 44.0
    T_MAX = 2 * SHIFT / (1 - SLOPE)

    x_v = x.rearrange("b (r p) n -> b p r n", p=P)
    out_v = out.rearrange("b (r p) n -> b p r n", p=P)

    ctx = ExitStack()
    with ctx:
        def sb(name, shape, dt=f32):
            return ctx.enter_context(nc.sbuf_tensor(name, shape, dt))

        def sem(name):
            return ctx.enter_context(nc.semaphore(name))

        ident = sb("ident", [P, P])
        ones_col = sb("ones_col", [P, 1])
        minus_half = sb("minus_half", [P, RT])
        neg_shift = sb("neg_shift", [P, 1])
        adj_off = sb("adj_off", [P, RT, C])
        bm_col = sb("bm_col", [P, RT])
        wcat = sb("wcat", [P, RT, CQ])
        wcat_hi = sb("wcat_hi", [P, RT, CQ], f32r)
        wcat_lo = sb("wcat_lo", [P, RT, CQ], f32r)
        stage_a = sb("stage_a", [P, FT, N])
        stage_b = sb("stage_b", [P, FT, N])
        wl_hi = sb("wl_hi", [P, FT, N], f32r)
        wl_lo = sb("wl_lo", [P, FT, N], f32r)
        wg_hi = sb("wg_hi", [P, FT, N], f32r)
        wg_lo = sb("wg_lo", [P, FT, N], f32r)
        m_hi = sb("m_hi", [P, FT, N], f32r)
        m_lo = sb("m_lo", [P, FT, N], f32r)
        gate_in = sb("gate_in", [P, 2])
        gate_exp = sb("gate_exp", [P, 2])
        gate_den = sb("gate_den", [P, 2])
        gate_inv = sb("gate_inv", [P, 2])
        xt = [sb(f"xt{p}", [P, RT, N]) for p in range(2)]
        x1 = [sb(f"x1_{p}", [P, RT, N]) for p in range(2)]
        stats = sb("stats", [P, 2, RT, 6])
        mean_var = sb("mean_var", [P, 2, RT, 2])
        var_eps = sb("var_eps", [P, 2, RT])
        rstd = sb("rstd", [P, 2, RT])
        shift = sb("shift", [P, 2, RT])
        h = sb("h", [P, RT, N])
        h_hi = sb("h_hi", [P, RT, N], f32r)
        h_lo = sb("h_lo", [P, RT, N], f32r)
        gt_hi = sb("gt_hi", [P, FT, C], f32r)
        gt_lo = sb("gt_lo", [P, FT, C], f32r)
        qk = sb("qk", [P, FT, 2])
        q_top = sb("q_top", [P, 1])
        q_max = sb("q_max", [P, 1])
        cols = sb("cols", [P, 2, FT])
        a_col = sb("a_col", [P, FT])
        b_col = sb("b_col", [P, FT])
        r_col = sb("r_col", [P, FT])
        r_row = sb("r_row", [P, N])
        pw = sb("pw", [P, FT, N])
        pw_hi = sb("pw_hi", [P, FT, N], f32r)
        pw_lo = sb("pw_lo", [P, FT, N], f32r)
        pair_sum = sb("pair_sum", [P, 2, N])
        pw_sum = sb("pw_sum", [P, N])
        rinv_col = sb("rinv_col", [P, FT])
        rinv_row = sb("rinv_row", [P, N])
        yn = sb("yn", [P, RT, N])
        result = sb("result", [P, RT, N])
        h2 = sb("h2", [P, RT, N])
        h2t_hi = sb("h2t_hi", [P, FT, C], f32r)
        h2t_lo = sb("h2t_lo", [P, FT, C], f32r)
        zl_hi = sb("zl_hi", [P, FT, C], f32r)
        zl_lo = sb("zl_lo", [P, FT, C], f32r)
        zg_hi = sb("zg_hi", [P, FT, C], f32r)
        zg_lo = sb("zg_lo", [P, FT, C], f32r)
        v_hi = sb("v_hi", [P, RT, N], f32r)
        v_lo = sb("v_lo", [P, RT, N], f32r)
        diag = sb("diag", [P, 4, P])
        sq = sb("sq", [P, 2, RT])
        sq_guard = sb("sq_guard", [P, RT])
        rnorm = sb("rnorm", [P, RT])
        norm_row = sb("norm_row", [P, 2, C])
        al = sb("al", [P, RT, C])
        dist = sb("dist", [P, RT, C])
        ag = sb("ag", [P, RT, C])
        kl = sb("kl", [P, RT, C])
        kg = sb("kg", [P, RT, C])
        kmat = sb("kmat", [P, RT, C])
        row_sum = sb("row_sum", [P, 2, RT])
        deg_scale = sb("deg_scale", [P, 2, RT])
        gate_coef = sb("gate_coef", [P, 2, RT])
        deg = sb("deg", [P, 2, RT])
        deg_guard = sb("deg_guard", [P, 2, RT])
        deg_inv = sb("deg_inv", [P, 2, RT])
        row_coef = sb("row_coef", [P, 2, RT])
        kt_hi = sb("kt_hi", [P, RT, C], f32r)
        kt_lo = sb("kt_lo", [P, RT, C], f32r)

        bank = [ctx.enter_context(nc.psum_tensor(f"bank{i}", [P, 512], f32)) for i in range(8)]
        GT_BANK = [4, 0, 1, 7]
        M_BANK = [0, 1, 5, 6]
        SUM_BANK, ROW_BANK, GL_BANK, GG_BANK, KT_BANK = 4, 7, 5, 6, 4

        wv_stage = [x1[1], result]
        wo_stage = [t[:, :, :].rearrange("p r c -> p (r c)") for t in (al, dist, ag, kl)]

        names = """weights_in adj_in small_in wlg_in wvo_in x_in0 x_in1 stored
            ident_zero ident_done consts_done adj_off_done wcat_split gate_exp_done gate_den_done
            gate_inv_done gate_coef_done wlg_hi wlg_lo m_done m_hi_done m_lo_done
            stats1 aggr1 var1 rstd1 shift1 h_done h_hi_done h_lo_done
            gt_done gt_hi_done qk_done gt_lo_done q_top_done q_row_done q_max_done cols_done
            exps_done r_row_done r_copied pw_done pw_hi_done pw_lo_done pair_done sum_done
            y_done sums_done rinv_done rinv_row_done rinv_copied yn_done relu_done x1_done
            stats2 aggr2 var2 rstd2 shift2 h2_done h2t_done h2t_hi_done h2t_lo_done
            zl_done zl_hi_done zl_lo_done zg_done zg_hi_done zg_lo_done
            gl_done gg_done sq_done guard_done rnorm_done norm_row_done norm_copied
            al_done dist_done dist2_done ag_done kl_done kg_done scale_done deg_done
            deg_guard_done deg_inv_done row_coef_done kg_scaled_done k_done
            kt_done kt_hi_done kt_lo_done v_done v_hi_done v_lo_done out_done added""".split()
        s = namedtuple("Semaphores", names)(*[sem(n) for n in names])
        x_in = [s.x_in0, s.x_in1]

        block = ctx.enter_context(nc.Block())
        TURNS = (B - 4) // 2

        def batch(n):
            return Batch(n, n % 2, n // 2)

        def f(t):
            return t.bitcast(f32)

        @block.sync
        def _(sp):
            def load_x(b):
                sp.dma_start(xt[b.p][:, :, :], x_v[b.n]).then_inc(x_in[b.p], 16)

            def load_next_x(b):
                sp.wait_ge(s.x1_done, RT * (b.n + 1))
                load_x(after(b, 2))

            def store(b):
                sp.wait_ge(s.added, RT * (b.n + 1))
                sp.dma_start(out_v[b.n], result[:, :, :]).then_inc(s.stored, 16)

            load_x(Batch(0, 0, 0))
            sp.dma_start(wcat[:, :, :], adj_wq_wk.rearrange("(r p) o -> p r o", p=P)).then_inc(s.weights_in, 16)
            sp.dma_start(bm_col[:, :], bm.rearrange("(r p) -> p r", p=P),
                         allow_slow_non_contiguous=True).then_inc(s.small_in, 16)
            load_x(Batch(1, 1, 0))
            sp.dma_start(gate_in[:, 0:1], gate_logit.partition_broadcast(P)).then_inc(s.small_in, 16)
            sp.dma_start(gate_in[:, 1:2], log_sigma.partition_broadcast(P)).then_inc(s.small_in, 16)
            for i, stage in enumerate(wv_stage):
                sp.dma_start(stage[:, :, :], wv.rearrange("(t p) d -> p t d", p=P)[:, 2 * i:2 * i + 2, :]).then_inc(s.wvo_in, 16)
            for k, stage in enumerate(wo_stage):
                sp.dma_start(stage, wo_t[k * P:(k + 1) * P, :]).then_inc(s.wvo_in, 16)
            sp.dma_start(stage_a[:, :, :], wl_t.rearrange("(t p) e -> p t e", p=P)).then_inc(s.wlg_in, 16)
            sp.dma_start(stage_b[:, :, :], wg_t.rearrange("(t p) e -> p t e", p=P)).then_inc(s.wlg_in, 16)
            sp.dma_start(adj_off[:, :, :], adj.rearrange("(r p) m -> p r m", p=P)).then_inc(s.adj_in, 16)
            for n in range(2):
                load_next_x(batch(n))
            with sp.Fori(0, TURNS) as i:
                for k in (1, 2):
                    b = Batch(2 * i + k, k % 2, i + k // 2)
                    store(after(b, -1))
                    load_next_x(after(b, 1))
            for n in range(2 * TURNS, B):
                store(batch(n))
            sp.wait_ge(s.stored, 1 + 16 * B)

        def run_batches(eng, turn):
            turn(batch(0), True, True, False)
            with eng.Fori(0, TURNS) as i:
                for k in (1, 2):
                    turn(Batch(2 * i + k, k % 2, i + k // 2), True, True, True)
            for n in range(2 * TURNS + 1, B):
                turn(batch(n), n + 1 < B, n + 2 < B, True)

        FIRST = batch(0)

        @block.tensor
        def _(pe):
            def product(dst, pairs):
                last = None
                for n, (lh, ll, rh, rl) in enumerate(pairs):
                    nc.tensor.matmul(dst, lh, rh, start=(n == 0), stop=False)
                    nc.tensor.matmul(dst, lh, rl, start=False, stop=False)
                    last = nc.tensor.matmul(dst, ll, rh, start=False, stop=(n == len(pairs) - 1))
                return last

            def row_of(dst, col):
                return nc.tensor.matmul(dst, col.broadcast_to((P, P)), ident[:, :], is_transpose=True,
                                        start=True, stop=True)

            def adj_h(c, values_before):
                pe.wait_ge(s.h_hi_done, c.n + 1)
                pe.wait_ge(s.h_lo_done, c.n + 1)
                for j in range(FT):
                    if values_before and j in (1, 2):
                        pe.wait_ge(s.v_lo_done, RT * (c.n - 2) + j)
                    if values_before and j == FT - 1:
                        pe.wait_ge(s.norm_copied, c.n - 1)
                    js = slice(j * P, (j + 1) * P)
                    product(bank[GT_BANK[j]][:, 0:CQ],
                            [(h_hi[:, r, js], h_lo[:, r, js], wcat_hi[:, r, :], wcat_lo[:, r, :])
                             for r in range(RT)]).then_inc(s.gt_done, 1)

            def max_q(c):
                pe.wait_ge(s.q_top_done, c.n + 1)
                pe.wait_ge(s.gt_lo_done, FT * (c.n + 1))
                row_of(bank[ROW_BANK][:, 0:P], q_top[:, 0:1]).then_inc(s.q_row_done, 1)

            def rows_r(c):
                pe.wait_ge(s.exps_done, 3 * (c.n + 1))
                for j in range(FT):
                    last = row_of(bank[ROW_BANK][:, j * P:(j + 1) * P], r_col[:, j:j + 1])
                last.then_inc(s.r_row_done, 1)

            def weighted(c, r):
                for j in range(FT):
                    if r == 0:
                        pe.wait_ge(s.pw_hi_done, FT * c.n + j + 1)
                        pe.wait_ge(s.pw_lo_done, FT * c.n + j + 1)
                    rs = slice(r * P, (r + 1) * P)
                    dst = bank[2 + r][:, :]
                    nc.tensor.matmul(dst, gt_hi[:, j, rs], pw_hi[:, j, :], start=(j == 0), stop=False)
                    nc.tensor.matmul(dst, gt_hi[:, j, rs], pw_lo[:, j, :], start=False, stop=False)
                    last = nc.tensor.matmul(dst, gt_lo[:, j, rs], pw_hi[:, j, :], start=False, stop=(j == FT - 1))
                last.then_inc(s.y_done, 1)

            def column_sums(c):
                pe.wait_ge(s.sum_done, c.n + 1)
                for j in range(FT):
                    last = nc.tensor.matmul(bank[SUM_BANK][:, j:j + 1], pw_sum[:, j * P:(j + 1) * P],
                                            ones_col[:, :], start=True, stop=True)
                last.then_inc(s.sums_done, 1)

            def rows_rinv(c):
                pe.wait_ge(s.rinv_done, c.n + 1)
                pe.wait_ge(s.r_copied, c.n + 1)
                for j in range(FT):
                    last = row_of(bank[ROW_BANK][:, j * P:(j + 1) * P], rinv_col[:, j:j + 1])
                last.then_inc(s.rinv_row_done, 1)

            def transpose_h2(c):
                pe.wait_ge(s.h2_done, RT * (c.n + 1))
                for half in range(2):
                    for t in range(2):
                        for r in range(RT):
                            d = 2 * half + t
                            last = nc.tensor.transpose(bank[2 + half][:, t * C + r * P:t * C + (r + 1) * P],
                                                       h2[:, r, d * P:(d + 1) * P], ident[:, :])
                    last.then_inc(s.h2t_done, 1)

            def project(b, w_hi, w_lo, done, banks, tiles):
                for e in tiles:
                    es = slice(e * P, (e + 1) * P)
                    last = product(bank[banks[e // 2]][:, (e % 2) * C:(e % 2 + 1) * C],
                                   [(w_hi[:, d, es], w_lo[:, d, es], h2t_hi[:, d, :], h2t_lo[:, d, :])
                                    for d in range(FT)])
                last.then_inc(done, 1)

            def gram(b, z_hi, z_lo, where, done):
                for r in range(RT):
                    rs = slice(r * P, (r + 1) * P)
                    last = product(bank[where][:, r * C:(r + 1) * C],
                                   [(z_hi[:, e, rs], z_lo[:, e, rs], z_hi[:, e, :], z_lo[:, e, :])
                                    for e in range(FT)])
                last.then_inc(done, 1)

            def rows_norms(b, layer0):
                if layer0:
                    pe.wait_ge(s.rinv_copied, b.n + 2)
                pe.wait_ge(s.rnorm_done, b.n + 1)
                pe.wait_ge(s.sq_done, 4 * (b.n + 1))
                for r in range(RT):
                    row_of(bank[ROW_BANK][:, r * P:(r + 1) * P], rnorm[:, r:r + 1])
                for r in range(RT):
                    last = row_of(bank[ROW_BANK][:, C + r * P:C + (r + 1) * P], sq[:, 1, r:r + 1])
                last.then_inc(s.norm_row_done, 1)

            def values(b, r):
                rs = slice(r * P, (r + 1) * P)
                product(bank[r][:, :], [(h2t_hi[:, d, rs], h2t_lo[:, d, rs], m_hi[:, d, :], m_lo[:, d, :])
                                        for d in range(FT)]).then_inc(s.v_done, 1)

            def transpose_k(b):
                pe.wait_ge(s.k_done, RT * (b.n + 1))
                for m in range(RT):
                    for r in range(RT):
                        last = nc.tensor.transpose(bank[KT_BANK][:, m * C + r * P:m * C + (r + 1) * P],
                                                   kmat[:, r, m * P:(m + 1) * P], ident[:, :])
                last.then_inc(s.kt_done, 1)

            def mix(b):
                pe.wait_ge(s.kt_lo_done, b.n + 1)
                pe.wait_ge(s.v_lo_done, RT * (b.n + 1))
                for r in range(RT):
                    rs = slice(r * P, (r + 1) * P)
                    product(bank[GL_BANK + r][:, :],
                            [(kt_hi[:, m, rs], kt_lo[:, m, rs], v_hi[:, m, :], v_lo[:, m, :])
                             for m in range(RT)]).then_inc(s.out_done, 1)

            pe.wait_ge(s.ident_done, 1)
            pe.wait_ge(s.consts_done, 2)
            pe.wait_ge(s.wcat_split, 2)
            adj_h(FIRST, False)
            max_q(FIRST)
            rows_r(FIRST)
            def make_m(tiles):
                for d in tiles:
                    for k in range(FT):
                        last = nc.tensor.matmul(bank[M_BANK[d]][:, :], wv_stage[k // 2][:, k % 2, d * P:(d + 1) * P],
                                                wo_stage[k], start=(k == 0), stop=(k == FT - 1))
                    last.then_inc(s.m_done, 1)

            pe.wait_ge(s.wvo_in, 96)
            make_m((0, 1))
            weighted(FIRST, 0)
            column_sums(FIRST)
            weighted(FIRST, 1)
            rows_rinv(FIRST)
            make_m((2, 3))
            pe.wait_ge(s.m_lo_done, 2)
            transpose_h2(FIRST)

            def turn(b, layer0, _, finish):
                c, e = after(b, 1), after(b, -1)
                if layer0:
                    adj_h(c, finish)
                pe.wait_ge(s.h2t_hi_done, 2 * (b.n + 1))
                pe.wait_ge(s.h2t_lo_done, 2 * (b.n + 1))
                if not finish:
                    pe.wait_ge(s.wlg_lo, 2)
                project(b, wl_hi, wl_lo, s.zl_done, (2, 3), (0, 1))
                if layer0:
                    max_q(c)
                project(b, wl_hi, wl_lo, s.zl_done, (2, 3), (2, 3))
                if layer0:
                    rows_r(c)
                if finish:
                    pe.wait_ge(s.v_lo_done, RT * b.n)
                project(b, wg_hi, wg_lo, s.zg_done, (0, 1), (0, 1))
                if finish:
                    transpose_k(e)
                project(b, wg_hi, wg_lo, s.zg_done, (0, 1), (2, 3))
                if finish:
                    mix(e)
                pe.wait_ge(s.zl_lo_done, 2 * (b.n + 1))
                if layer0:
                    weighted(c, 0)
                    column_sums(c)
                    weighted(c, 1)
                    rows_rinv(c)
                if finish:
                    pe.wait_ge(s.added, RT * b.n)
                else:
                    pe.wait_ge(s.m_lo_done, FT)
                gram(b, zl_hi, zl_lo, GL_BANK, s.gl_done)
                pe.wait_ge(s.zg_lo_done, 2 * (b.n + 1))
                gram(b, zg_hi, zg_lo, GG_BANK, s.gg_done)
                values(b, 0)
                rows_norms(b, layer0)
                values(b, 1)
                if layer0:
                    transpose_h2(c)

            run_batches(pe, turn)
            transpose_k(batch(B - 1))
            mix(batch(B - 1))

        @block.scalar
        def _(act):
            def normalised(b, src, done, which, ready):
                act.wait_ge(ready, b.n + 1)
                for r in range(RT):
                    nc.scalar.activation(done[0][:, r, :], src[:, r, :], ACT.Relu,
                                         bias=shift[:, which, r:r + 1],
                                         scale=rstd[:, which, r:r + 1]).then_inc(done[1], 1)

            def high_h(a):
                act.wait_ge(s.h_done, RT * (a.n + 1))
                nc.scalar.copy(h_hi[:, :, :], h[:, :, :]).then_inc(s.h_hi_done, 1)

            def high_gt(c):
                for j in range(FT):
                    act.wait_ge(s.gt_done, FT * c.n + j + 1)
                    nc.scalar.copy(gt_hi[:, j, :], bank[GT_BANK[j]][:, 0:C]).then_inc(s.gt_hi_done, 1)

            def exps(c):
                act.wait_ge(s.cols_done, 2 * (c.n + 1))
                nc.scalar.activation(r_col[:, :], cols[:, 1, :], ACT.Exp, bias=neg_shift[:, 0:1],
                                     scale=1 - SLOPE).then_inc(s.exps_done, 1)
                nc.scalar.activation(a_col[:, :], cols[:, 0, :], ACT.Exp).then_inc(s.exps_done, 1)
                nc.scalar.activation(b_col[:, :], cols[:, 0, :], ACT.Exp, bias=neg_shift[:, 0:1],
                                     scale=SLOPE).then_inc(s.exps_done, 1)

            def copy_r(c):
                act.wait_ge(s.r_row_done, c.n + 1)
                nc.scalar.copy(r_row[:, :], bank[ROW_BANK][:, :]).then_inc(s.r_copied, 1)

            def high_pw(c):
                for j in range(FT):
                    act.wait_ge(s.pw_done, FT * c.n + j + 1)
                    nc.scalar.copy(pw_hi[:, j, :], pw[:, j, :]).then_inc(s.pw_hi_done, 1)

            def copy_rinv(c):
                act.wait_ge(s.rinv_row_done, c.n + 1)
                nc.scalar.copy(rinv_row[:, :], bank[ROW_BANK][:, :]).then_inc(s.rinv_copied, 1)

            def relu_y(c):
                for r in range(RT):
                    act.wait_ge(s.yn_done, RT * c.n + r + 1)
                    nc.scalar.activation(yn[:, r, :], yn[:, r, :], ACT.Relu,
                                         bias=bm_col[:, r:r + 1]).then_inc(s.relu_done, 1)

            def high(wait_on, count, dst, src, done):
                act.wait_ge(wait_on, count)
                nc.scalar.copy(dst, src).then_inc(done, 1)

            def two_tiles(t, i):
                return t[:, 2 * i:2 * i + 2, :].rearrange("p t c -> p (t c)")

            def high_kt(b):
                high(s.kt_done, b.n + 1, kt_hi[:, :, :].rearrange("p r c -> p (r c)"), bank[KT_BANK][:, :],
                     s.kt_hi_done)

            def high_h2t(c):
                for i in range(2):
                    high(s.h2t_done, 2 * c.n + i + 1, two_tiles(h2t_hi, i), bank[2 + i][:, :], s.h2t_hi_done)

            def high_m(d):
                high(s.m_done, d + 1, m_hi[:, d, :], bank[M_BANK[d]][:, :], s.m_hi_done)

            act.wait_ge(s.consts_done, 2)
            act.wait_ge(s.weights_in, 16)
            nc.scalar.copy(wcat_hi[:, :, :], wcat[:, :, :]).then_inc(s.wcat_split, 1)
            normalised(FIRST, xt[0], (h, s.h_done), 0, s.shift1)
            high_h(FIRST)
            act.wait_ge(s.small_in, 48)
            nc.scalar.activation(gate_exp[:, 0:1], gate_in[:, 0:1], ACT.Exp, scale=-1.0).then_inc(s.gate_exp_done, 1)
            nc.scalar.activation(gate_exp[:, 1:2], gate_in[:, 1:2], ACT.Exp).then_inc(s.gate_exp_done, 1)
            high_gt(FIRST)
            exps(FIRST)
            copy_r(FIRST)
            high_pw(FIRST)
            act.wait_ge(s.h_lo_done, 1)
            act.wait_ge(s.gt_done, FT)
            normalised(after(FIRST, 1), xt[1], (h, s.h_done), 0, s.shift1)
            high_h(after(FIRST, 1))
            high_m(0)
            high_m(1)
            act.wait_ge(s.wlg_in, 32)
            nc.scalar.copy(wl_hi[:, :, :], stage_a[:, :, :]).then_inc(s.wlg_hi, 1)
            copy_rinv(FIRST)
            relu_y(FIRST)
            nc.scalar.copy(wg_hi[:, :, :], stage_b[:, :, :]).then_inc(s.wlg_hi, 1)
            high_m(2)
            normalised(FIRST, x1[0], (h2, s.h2_done), 1, s.shift2)
            high_m(3)
            high_h2t(FIRST)

            def turn(b, layer0, norm0, finish):
                c, a, e = after(b, 1), after(b, 2), after(b, -1)
                if layer0:
                    high_gt(c)
                high(s.zl_done, 2 * b.n + 1, two_tiles(zl_hi, 0), bank[2][:, :], s.zl_hi_done)
                if layer0:
                    exps(c)
                high(s.zl_done, 2 * b.n + 2, two_tiles(zl_hi, 1), bank[3][:, :], s.zl_hi_done)
                if layer0:
                    copy_r(c)
                    high_pw(c)
                high(s.zg_done, 2 * b.n + 1, two_tiles(zg_hi, 0), bank[0][:, :], s.zg_hi_done)
                if finish:
                    high_kt(e)
                high(s.zg_done, 2 * b.n + 2, two_tiles(zg_hi, 1), bank[1][:, :], s.zg_hi_done)
                if norm0:
                    normalised(a, xt[a.p], (h, s.h_done), 0, s.shift1)
                    high_h(a)
                if layer0:
                    copy_rinv(c)
                    relu_y(c)
                    normalised(c, x1[c.p], (h2, s.h2_done), 1, s.shift2)
                high(s.v_done, RT * b.n + 1, v_hi[:, 0, :], bank[0][:, :], s.v_hi_done)
                high(s.norm_row_done, b.n + 1, norm_row[:, :, :].rearrange("p s c -> p (s c)"),
                     bank[ROW_BANK][:, :], s.norm_copied)
                high(s.v_done, RT * b.n + 2, v_hi[:, 1, :], bank[1][:, :], s.v_hi_done)
                if layer0:
                    high_h2t(c)
                act.wait_ge(s.dist2_done, RT * (b.n + 1))
                nc.scalar.activation(ag[:, :, :], dist[:, :, :], ACT.Exp,
                                     scale=gate_inv[:, 1:2]).then_inc(s.ag_done, 1)

            run_batches(act, turn)
            high_kt(batch(B - 1))

        @block.gpsimd
        def _(pool):
            def power(dst, src, ready, count, done):
                pool.wait_ge(ready, count)
                nc.gpsimd.tensor_tensor(dst, src, minus_half[:, :], ALU.pow).then_inc(done, 1)

            def sum_pw(c):
                pool.wait_ge(s.pw_done, FT * (c.n + 1))
                nc.gpsimd.tensor_tensor(pair_sum[:, :, :], pw[:, 0:2, :], pw[:, 2:4, :], ALU.add).then_inc(s.pair_done, 1)
                pool.wait_ge(s.pair_done, c.n + 1)
                nc.gpsimd.tensor_tensor(pw_sum[:, :], pair_sum[:, 0, :], pair_sum[:, 1, :], ALU.add).then_inc(s.sum_done, 1)

            def residual(c, result_before):
                if result_before:
                    pool.wait_ge(s.added, RT * (c.n - 1))
                for r in range(RT):
                    pool.wait_ge(s.relu_done, RT * c.n + r + 1)
                    nc.gpsimd.tensor_tensor(x1[c.p][:, r, :], xt[c.p][:, r, :], yn[:, r, :], ALU.add).then_inc(s.x1_done, 1)

            nc.gpsimd.memset(minus_half[:, :], -0.5).then_inc(s.consts_done, 1)
            nc.gpsimd.memset(ident[:, :], 0.0).then_inc(s.ident_zero, 1)
            pool.wait_ge(s.ident_zero, 1)
            nc.gpsimd.affine_select(out=ident[:, :], in_=ident[:, :], compare_op=ALU.not_equal, fill=1.0, base=0,
                                    pattern=[[-1, P]], channel_multiplier=1).then_inc(s.ident_done, 1)
            pool.wait_ge(s.consts_done, 2)
            power(rstd[:, 0, :], var_eps[:, 0, :], s.var1, 1, s.rstd1)
            pool.wait_ge(s.adj_in, 16)
            nc.gpsimd.affine_select(out=adj_off[:, :, :], in_=adj_off[:, :, :], compare_op=ALU.not_equal, fill=0.0,
                                    base=0, pattern=[[P, RT], [-1, C]], channel_multiplier=1).then_inc(s.adj_off_done, 1)
            power(rstd[:, 0, :], var_eps[:, 0, :], s.var1, 2, s.rstd1)
            sum_pw(FIRST)
            residual(FIRST, False)
            power(rstd[:, 1, :], var_eps[:, 1, :], s.var2, 1, s.rstd2)

            def turn(b, layer0, norm0, finish):
                c, a = after(b, 1), after(b, 2)
                if layer0:
                    sum_pw(c)
                if norm0:
                    power(rstd[:, 0, :], var_eps[:, 0, :], s.var1, a.n + 1, s.rstd1)
                if layer0:
                    residual(c, finish)
                power(rnorm[:, :], sq_guard[:, :], s.guard_done, b.n + 1, s.rnorm_done)
                if layer0:
                    power(rstd[:, 1, :], var_eps[:, 1, :], s.var2, c.n + 1, s.rstd2)

            run_batches(pool, turn)

        @block.vector
        def _(dve):
            def low(wait_on, count, dst, src, hi, done):
                dve.wait_ge(wait_on, count)
                nc.vector.tensor_tensor(dst, src, f(hi), ALU.subtract).then_inc(done, 1)

            def statistics(b, src, which, src_ready, counts, stat_sem):
                for r in range(RT):
                    dve.wait_ge(src_ready, counts[r])
                    nc.vector.bn_stats(stats[:, which, r, :], src[:, r, :]).then_inc(stat_sem, 1)
                dve.wait_ge(stat_sem, RT * (b.n + 1))

            def aggregate(b, which, aggr_sem, var_sem):
                for r in range(RT):
                    nc.vector.bn_aggr(mean_var[:, which, r, :], stats[:, which, r, :]).then_inc(aggr_sem, 1)
                dve.wait_ge(aggr_sem, RT * (b.n + 1))
                nc.vector.tensor_scalar(var_eps[:, which, :], mean_var[:, which, :, 1], LN_EPS, None,
                                        ALU.add).then_inc(var_sem, 1)

            def statistics1(a):
                statistics(a, xt[a.p], 0, x_in[a.p], [16 * (a.half + 1)] * RT, s.stats1)

            def aggregate1(a):
                aggregate(a, 0, s.aggr1, s.var1)

            def statistics2(c):
                statistics(c, x1[c.p], 1, s.x1_done, [RT * c.n + r + 1 for r in range(RT)], s.stats2)

            def aggregate2(c):
                aggregate(c, 1, s.aggr2, s.var2)

            def minus_mean_rstd(b, which, rstd_sem, shift_sem):
                dve.wait_ge(rstd_sem, b.n + 1)
                nc.vector.scalar_tensor_tensor(out=shift[:, which, :], in0=mean_var[:, which, :, 0], scalar=-1.0,
                                               in1=rstd[:, which, :], op0=ALU.mult, op1=ALU.mult).then_inc(shift_sem, 1)

            def low_gt(c):
                for j in range(FT):
                    dve.wait_ge(s.gt_hi_done, FT * c.n + j + 1)
                    nc.vector.tensor_copy(qk[:, j, :], bank[GT_BANK[j]][:, C:CQ]).then_inc(s.qk_done, 1)
                    nc.vector.tensor_tensor(gt_lo[:, j, :], bank[GT_BANK[j]][:, 0:C], f(gt_hi[:, j, :]),
                                            ALU.subtract).then_inc(s.gt_lo_done, 1)
                dve.wait_ge(s.qk_done, FT * (c.n + 1))
                nc.vector.reduce_max(q_top[:, :], qk[:, :, 0], AX_X).then_inc(s.q_top_done, 1)

            def columns(c):
                dve.wait_ge(s.q_row_done, c.n + 1)
                nc.vector.reduce_max(q_max[:, :], bank[ROW_BANK][:, 0:P], AX_X).then_inc(s.q_max_done, 1)
                dve.wait_ge(s.q_max_done, c.n + 1)
                nc.vector.tensor_scalar(cols[:, 1, :], qk[:, :, 1], q_max[:, 0:1], T_MAX, ALU.add,
                                        ALU.min).then_inc(s.cols_done, 1)
                nc.vector.tensor_scalar(cols[:, 0, :], qk[:, :, 0], q_max[:, 0:1], None,
                                        ALU.subtract).then_inc(s.cols_done, 1)

            def weights_p(c):
                dve.wait_ge(s.r_copied, c.n + 1)
                dve.wait_ge(s.exps_done, 3 * (c.n + 1))
                for j in range(FT):
                    nc.vector.tensor_scalar(pw[:, j, :], r_row[:, :], a_col[:, j:j + 1], b_col[:, j:j + 1],
                                            ALU.mult, ALU.max).then_inc(s.pw_done, 1)

            def low_p(c, first, end):
                for j in range(first, end):
                    low(s.pw_hi_done, FT * c.n + j + 1, pw_lo[:, j, :], pw[:, j, :], pw_hi[:, j, :], s.pw_lo_done)

            def invert_sums(c):
                dve.wait_ge(s.sums_done, c.n + 1)
                nc.vector.reciprocal(rinv_col[:, :], bank[SUM_BANK][:, 0:FT]).then_inc(s.rinv_done, 1)

            def normalise_y(c):
                dve.wait_ge(s.rinv_copied, c.n + 1)
                for r in range(RT):
                    dve.wait_ge(s.y_done, RT * c.n + r + 1)
                    nc.vector.tensor_tensor(yn[:, r, :], bank[2 + r][:, :], rinv_row[:, :], ALU.mult).then_inc(s.yn_done, 1)

            def two_tiles(t, i):
                return t[:, 2 * i:2 * i + 2, :].rearrange("p t c -> p (t c)")

            def low_h2t(c):
                for i in range(2):
                    low(s.h2t_hi_done, 2 * c.n + i + 1, two_tiles(h2t_lo, i), bank[2 + i][:, :],
                        two_tiles(h2t_hi, i), s.h2t_lo_done)

            def squared_norms(b, g, where, ready):
                dve.wait_ge(ready, b.n + 1)
                for r in range(RT):
                    at = r * C + r * P
                    nc.vector.tensor_tensor_reduce(
                        out=diag[:, 2 * g + r, :], in0=bank[where][:, at:at + P], in1=ident[:, :], scale=1.0,
                        scalar=0.0, op0=ALU.mult, op1=ALU.add, accum_out=sq[:, g, r:r + 1]).then_inc(s.sq_done, 1)

            def guard_norms(b):
                dve.wait_ge(s.sq_done, 4 * b.n + RT)
                nc.vector.tensor_scalar(sq_guard[:, :], sq[:, 0, :], NORM_EPS * NORM_EPS, None,
                                        ALU.max).then_inc(s.guard_done, 1)

            def kernels(b):
                dve.wait_ge(s.norm_copied, b.n + 1)
                dve.wait_ge(s.sq_done, 4 * (b.n + 1))
                gg = bank[GG_BANK][:, :].rearrange("p (r c) -> p r c", r=RT)
                gl = bank[GL_BANK][:, :].rearrange("p (r c) -> p r c", r=RT)
                nc.vector.scalar_tensor_tensor(
                    out=dist[:, :, :], in0=gg, scalar=-2.0, in1=norm_row[:, 1:2, :].broadcast_to((P, RT, C)),
                    op0=ALU.mult, op1=ALU.add).then_inc(s.dist_done, 1)
                nc.vector.scalar_tensor_tensor(
                    out=al[:, :, :], in0=gl, scalar=0.0, in1=norm_row[:, 0:1, :].broadcast_to((P, RT, C)),
                    op0=ALU.max, op1=ALU.mult).then_inc(s.al_done, 1)
                dve.wait_ge(s.dist_done, b.n + 1)
                for r in range(RT):
                    nc.vector.tensor_scalar(dist[:, r, :], dist[:, r, :], sq[:, 1, r:r + 1], 0.0, ALU.add,
                                            ALU.max).then_inc(s.dist2_done, 1)

            def masked(b, src, ready, count, dst, g, done):
                dve.wait_ge(ready, count)
                for r in range(RT):
                    nc.vector.tensor_tensor_reduce(
                        out=dst[:, r, :], in0=src[:, r, :], in1=adj_off[:, r, :], scale=1.0, scalar=0.0,
                        op0=ALU.mult, op1=ALU.add, accum_out=row_sum[:, g, r:r + 1]).then_inc(done, 1)

            def row_scales(b):
                nc.vector.tensor_copy(deg_scale[:, 0, :], rnorm[:, :]).then_inc(s.scale_done, 1)
                nc.vector.tensor_scalar(gate_coef[:, 0, :], rnorm[:, :], gate_inv[:, 0:1], None,
                                        ALU.mult).then_inc(s.scale_done, 1)

            def combine(b):
                dve.wait_ge(s.kl_done, RT * (b.n + 1))
                dve.wait_ge(s.kg_done, RT * (b.n + 1))
                dve.wait_ge(s.scale_done, 2 * (b.n + 1))
                nc.vector.tensor_tensor(deg[:, :, :], row_sum[:, :, :], deg_scale[:, :, :], ALU.mult).then_inc(s.deg_done, 1)
                dve.wait_ge(s.deg_done, b.n + 1)
                nc.vector.tensor_scalar(deg_guard[:, :, :], deg[:, :, :], DEG_EPS, None, ALU.max).then_inc(s.deg_guard_done, 1)
                dve.wait_ge(s.deg_guard_done, b.n + 1)
                nc.vector.reciprocal(deg_inv[:, :, :], deg_guard[:, :, :]).then_inc(s.deg_inv_done, 1)
                dve.wait_ge(s.deg_inv_done, b.n + 1)
                nc.vector.tensor_tensor(row_coef[:, :, :], deg_inv[:, :, :], gate_coef[:, :, :], ALU.mult).then_inc(s.row_coef_done, 1)
                dve.wait_ge(s.row_coef_done, b.n + 1)
                for r in range(RT):
                    nc.vector.tensor_scalar(dist[:, r, :], kg[:, r, :], row_coef[:, 1, r:r + 1], None,
                                            ALU.mult).then_inc(s.kg_scaled_done, 1)
                for r in range(RT):
                    dve.wait_ge(s.kg_scaled_done, RT * b.n + r + 1)
                    nc.vector.scalar_tensor_tensor(
                        out=kmat[:, r, :], in0=kl[:, r, :], scalar=row_coef[:, 0, r:r + 1], in1=dist[:, r, :],
                        op0=ALU.mult, op1=ALU.add).then_inc(s.k_done, 1)

            def low_v(b, r):
                low(s.v_hi_done, RT * b.n + r + 1, v_lo[:, r, :], bank[r][:, :], v_hi[:, r, :], s.v_lo_done)

            def low_kt(b):
                low(s.kt_hi_done, b.n + 1, kt_lo[:, :, :].rearrange("p r c -> p (r c)"), bank[KT_BANK][:, :],
                    kt_hi[:, :, :].rearrange("p r c -> p (r c)"), s.kt_lo_done)

            def add_result(b):
                dve.wait_ge(s.stored, 1 + 16 * b.n)
                for r in range(RT):
                    dve.wait_ge(s.out_done, RT * b.n + r + 1)
                    nc.vector.tensor_tensor(result[:, r, :], bank[GL_BANK + r][:, :], x1[b.p][:, r, :],
                                            ALU.add).then_inc(s.added, 1)

            def low_m(d):
                low(s.m_hi_done, d + 1, m_lo[:, d, :], bank[M_BANK[d]][:, :], m_hi[:, d, :], s.m_lo_done)

            nc.vector.memset(neg_shift[:, :], -SHIFT).then_inc(s.stored, 1)
            nc.vector.memset(deg_scale[:, 1, :], 1.0)
            nc.vector.memset(ones_col[:, :], 1.0).then_inc(s.consts_done, 1)
            dve.wait_ge(s.consts_done, 2)
            statistics1(FIRST)
            aggregate1(FIRST)
            low(s.wcat_split, 1, wcat_lo[:, :, :], wcat[:, :, :], wcat_hi[:, :, :], s.wcat_split)
            minus_mean_rstd(FIRST, 0, s.rstd1, s.shift1)
            low(s.h_hi_done, 1, h_lo[:, :, :], h[:, :, :], h_hi[:, :, :], s.h_lo_done)
            dve.wait_ge(s.gate_exp_done, 2)
            nc.vector.tensor_scalar(gate_den[:, 0:1], gate_exp[:, 0:1], 1.0, None, ALU.add).then_inc(s.gate_den_done, 1)
            nc.vector.tensor_scalar(gate_den[:, 1:2], gate_exp[:, 1:2], gate_exp[:, 1:2], -2.0, ALU.mult,
                                    ALU.mult).then_inc(s.gate_den_done, 1)
            dve.wait_ge(s.gate_den_done, 2)
            nc.vector.reciprocal(gate_inv[:, :], gate_den[:, :]).then_inc(s.gate_inv_done, 1)
            dve.wait_ge(s.gate_inv_done, 1)
            for r in range(RT):
                nc.vector.tensor_scalar(gate_coef[:, 1, r:r + 1], gate_inv[:, 0:1], -1.0, 1.0, ALU.mult,
                                        ALU.add).then_inc(s.gate_coef_done, 1)
            low_gt(FIRST)
            columns(FIRST)
            weights_p(FIRST)
            low_p(FIRST, 0, FT)
            statistics1(after(FIRST, 1))
            aggregate1(after(FIRST, 1))
            minus_mean_rstd(after(FIRST, 1), 0, s.rstd1, s.shift1)
            low(s.h_hi_done, 2, h_lo[:, :, :], h[:, :, :], h_hi[:, :, :], s.h_lo_done)
            low_m(0)
            low_m(1)
            low(s.wlg_hi, 1, wl_lo[:, :, :], stage_a[:, :, :], wl_hi[:, :, :], s.wlg_lo)
            invert_sums(FIRST)
            normalise_y(FIRST)
            statistics2(FIRST)
            aggregate2(FIRST)
            minus_mean_rstd(FIRST, 1, s.rstd2, s.shift2)
            low_m(2)
            low(s.wlg_hi, 2, wg_lo[:, :, :], stage_b[:, :, :], wg_hi[:, :, :], s.wlg_lo)
            low_m(3)
            low_h2t(FIRST)
            dve.wait_ge(s.adj_off_done, 1)
            dve.wait_ge(s.gate_coef_done, 2)

            def make_k(b, c):
                masked(b, al, s.al_done, b.n + 1, kl, 0, s.kl_done)
                masked(b, ag, s.ag_done, b.n + 1, kg, 1, s.kg_done)
                row_scales(b)
                if c is not None:
                    columns(c)
                combine(b)

            def turn(b, layer0, norm0, finish):
                c, a, e = after(b, 1), after(b, 2), after(b, -1)
                if layer0:
                    low_gt(c)
                if finish:
                    make_k(e, c if layer0 else None)
                else:
                    columns(c)
                low(s.zl_hi_done, 2 * b.n + 1, two_tiles(zl_lo, 0), bank[2][:, :], two_tiles(zl_hi, 0), s.zl_lo_done)
                if layer0:
                    weights_p(c)
                low(s.zl_hi_done, 2 * b.n + 2, two_tiles(zl_lo, 1), bank[3][:, :], two_tiles(zl_hi, 1), s.zl_lo_done)
                if layer0:
                    low_p(c, 0, 2)
                if finish:
                    low_kt(e)
                if layer0:
                    low_p(c, 2, FT)
                if norm0:
                    statistics1(a)
                low(s.zg_hi_done, 2 * b.n + 1, two_tiles(zg_lo, 0), bank[0][:, :], two_tiles(zg_hi, 0), s.zg_lo_done)
                if norm0:
                    aggregate1(a)
                low(s.zg_hi_done, 2 * b.n + 2, two_tiles(zg_lo, 1), bank[1][:, :], two_tiles(zg_hi, 1), s.zg_lo_done)
                if norm0:
                    minus_mean_rstd(a, 0, s.rstd1, s.shift1)
                if layer0:
                    invert_sums(c)
                if finish:
                    add_result(e)
                if norm0:
                    low(s.h_hi_done, a.n + 1, h_lo[:, :, :], h[:, :, :], h_hi[:, :, :], s.h_lo_done)
                if layer0:
                    normalise_y(c)
                squared_norms(b, 0, GL_BANK, s.gl_done)
                guard_norms(b)
                if layer0:
                    statistics2(c)
                squared_norms(b, 1, GG_BANK, s.gg_done)
                if layer0:
                    aggregate2(c)
                    minus_mean_rstd(c, 1, s.rstd2, s.shift2)
                low_v(b, 0)
                kernels(b)
                low_v(b, 1)
                if layer0:
                    low_h2t(c)

            run_batches(dve, turn)
            make_k(batch(B - 1), None)
            low_kt(batch(B - 1))
            add_result(batch(B - 1))


def kernel(**inputs):
    import numpy as np
    import concourse.bacc as bacc
    from concourse import mybir as mb
    from concourse.bass_utils import run_bass_kernel_spmd

    given = {name: np.asarray(a) for name, a in inputs.items()}
    laid = {
        "x": given["x"],
        "adj": given["adj"],
        "adj_wq_wk": np.concatenate([given["adj"].T, given["L0_gnn_wq"][:, None], given["L0_gnn_wk"][:, None]], axis=1),
        "bm": given["L0_gnn_bm"],
        "wl_t": given["L1_gnn_W_lang"].T,
        "wg_t": given["L1_gnn_W_grav"].T,
        "wv": given["L1_gnn_W_V"],
        "wo_t": given["L1_gnn_W_O"].T,
        "gate_logit": given["L1_gnn_gate_logit"].reshape(1),
        "log_sigma": given["L1_gnn_log_sigma"].reshape(1),
    }
    nc = bacc.Bacc("TRN2", target_bir_lowering=False, num_devices=1)
    arrays, args = {}, []
    for name, a in laid.items():
        arrays[f"in_{name}"] = np.ascontiguousarray(a)
        args.append(nc.dram_tensor(f"in_{name}", a.shape, mb.dt.from_np(a.dtype), kind="ExternalInput").ap())
    args.append(nc.dram_tensor("out_x", given["x"].shape, mb.dt.float32, kind="ExternalOutput").ap())
    graph_layers_kernel(nc, *args)
    r = run_bass_kernel_spmd(nc, [arrays], core_ids=[0])
    return r.results[0]["out_x"]
```

```python
from collections import namedtuple
from contextlib import ExitStack

import concourse.bass as bass
from concourse import mybir

Batch = namedtuple("Batch", "n p half")


def after(b, k):
    return Batch(b.n + k, (b.p + k) % 2, b.half + (b.p + k) // 2)


def graph_layers_kernel(nc, x, adj, adj_wq_wk, bm, wl, wg, wv, wo_t, gate_logit, log_sigma, out):
    f32 = mybir.dt.float32
    f32r = mybir.dt.float32r
    ALU = mybir.AluOpType
    ACT = mybir.ActivationFunctionType
    AX_X = mybir.AxisListType.X

    B, C, N = x.shape
    P = 128
    RT = C // P
    FT = N // P
    CQ = C + 2
    LN_EPS = 1e-5
    DEG_EPS = 1e-8
    NORM_EPS = 1e-8
    SLOPE = 0.01
    SHIFT = 44.0
    T_MAX = 2 * SHIFT / (1 - SLOPE)

    x_v = x.rearrange("b (r p) n -> b p r n", p=P)
    out_v = out.rearrange("b (r p) n -> b p r n", p=P)

    ctx = ExitStack()
    with ctx:
        def sb(name, shape, dt=f32):
            return ctx.enter_context(nc.sbuf_tensor(name, shape, dt))

        def sem(name):
            return ctx.enter_context(nc.semaphore(name))

        ident = sb("ident", [P, P])
        tri = sb("tri", [P, P])
        minus_half = sb("minus_half", [P, RT])
        neg_shift = sb("neg_shift", [P, 1])
        adj_off = sb("adj_off", [P, RT, C])
        bm_col = sb("bm_col", [P, RT])
        wcat = sb("wcat", [P, RT, CQ])
        wcat_hi = sb("wcat_hi", [P, RT, CQ], f32r)
        wcat_lo = sb("wcat_lo", [P, RT, CQ], f32r)
        stage_a = sb("stage_a", [P, FT, N])
        stage_b = sb("stage_b", [P, FT, N])
        ul_hi = sb("ul_hi", [P, FT, N], f32r)
        ul_lo = sb("ul_lo", [P, FT, N], f32r)
        ug_hi = sb("ug_hi", [P, FT, N], f32r)
        ug_lo = sb("ug_lo", [P, FT, N], f32r)
        m_hi = sb("m_hi", [P, FT, N], f32r)
        m_lo = sb("m_lo", [P, FT, N], f32r)
        gate_in = sb("gate_in", [P, 2])
        gate_exp = sb("gate_exp", [P, 2])
        gate_den = sb("gate_den", [P, 2])
        gate_inv = sb("gate_inv", [P, 2])
        xt = [sb(f"xt{p}", [P, RT, N]) for p in range(2)]
        x1 = [sb(f"x1_{p}", [P, RT, N]) for p in range(2)]
        stats = sb("stats", [P, 2, RT, 6])
        mean_var = sb("mean_var", [P, 2, RT, 2])
        var_eps = sb("var_eps", [P, 2, RT])
        rstd = sb("rstd", [P, 2, RT])
        shift = sb("shift", [P, 2, RT])
        h = sb("h", [P, RT, N])
        h_hi = sb("h_hi", [P, RT, N], f32r)
        h_lo = sb("h_lo", [P, RT, N], f32r)
        gt_hi = sb("gt_hi", [P, FT, C + 2], f32r)
        gt_lo = sb("gt_lo", [P, FT, C + 2], f32r)
        qk = sb("qk", [P, FT, 2])
        q_top = sb("q_top", [P, 1])
        q_max = sb("q_max", [P, 1])
        cols = sb("cols", [P, 2, FT])
        a_col = sb("a_col", [P, FT])
        b_col = sb("b_col", [P, FT])
        r_col = sb("r_col", [P, FT])
        r_row = sb("r_row", [P, N])
        pw = sb("pw", [P, FT, N])
        pw_hi = sb("pw_hi", [P, FT, N], f32r)
        pw_lo = sb("pw_lo", [P, FT, N], f32r)
        rinv_col = sb("rinv_col", [P, FT])
        yt = sb("yt", [P, FT, C])
        yn = sb("yn", [P, RT, N])
        result = sb("result", [P, RT, N])
        h2 = sb("h2", [P, RT, N])
        h2t_hi = sb("h2t_hi", [P, FT, C], f32r)
        h2t_lo = sb("h2t_lo", [P, FT, C], f32r)
        t_hi = sb("t_hi", [P, FT, 2, C], f32r)
        t_lo = sb("t_lo", [P, FT, 2, C], f32r)
        v_hi = [sb(f"v_hi{i}", [P, N], f32r) for i in range(3)]
        v_lo = [sb(f"v_lo{i}", [P, N], f32r) for i in range(3)]
        diag = sb("diag", [P, 4, P])
        sq = sb("sq", [P, 2, RT])
        sq_guard = sb("sq_guard", [P, RT])
        rnorm = sb("rnorm", [P, RT])
        al = sb("al", [P, RT, C])
        dist = sb("dist", [P, RT, C])
        ag = sb("ag", [P, RT, C])
        kl = sb("kl", [P, RT, C])
        row_sum = sb("row_sum", [P, 2, RT])
        deg_scale = sb("deg_scale", [P, 2, RT])
        gate_coef = sb("gate_coef", [P, 2, RT])
        deg = sb("deg", [P, 2, RT])
        deg_guard = sb("deg_guard", [P, 2, RT])
        deg_inv = sb("deg_inv", [P, 2, RT])
        row_coef = sb("row_coef", [P, 2, RT])
        kt_hi = sb("kt_hi", [P, RT, C], f32r)
        kt_lo = sb("kt_lo", [P, RT, C], f32r)

        bank = [ctx.enter_context(nc.psum_tensor(f"bank{i}", [P, 512], f32)) for i in range(8)]
        GT_BANK = [4, 0, 1, 7]
        U_BANK = [2, 3, 5, 6]
        M_BANK = [0, 1, 5, 6]
        YT_BANK = [2, 3, 4, 7]
        Y_BANK = H2T_BANK = TL_BANK = [2, 3]
        V_BANK = TG_BANK = [0, 1]
        S_BANK = [5, 6]
        ROW_BANK, KT_BANK = 7, 4
        OUT_BANK, LAST_OUT_BANK = S_BANK, [2, 3]

        def two_tiles(t, i):
            return t[:, 2 * i:2 * i + 2, :].rearrange("p t c -> p (t c)")

        def in_two(i):
            return bank[i][:, :].rearrange("p (t c) -> p t c", c=C)

        def both_kinds(t, d):
            return t[:, d, :, :].rearrange("p k c -> p (k c)")

        s_rows, gram = stage_a[:, 0:RT, :], stage_a[:, RT:2 * RT, :]

        kmat, kg, norm_row = (stage_b[:, t, :].rearrange("p (r c) -> p r c", c=C) for t in range(3))

        wv_stage = [x1[1], result]
        wo_stage = [t[:, :, :].rearrange("p r c -> p (r c)") for t in (al, dist, ag, kl)]

        wv_hi, wv_lo = ([both_kinds(t, d) for d in range(FT)] for t in (t_hi, t_lo))
        wo_hi, wo_lo = ([t[:, :] for t in v] + [kt[:, :, :].rearrange("p r c -> p (r c)")]
                        for v, kt in ((v_hi, kt_hi), (v_lo, kt_lo)))

        names = """weights_in adj_in small_in wl_in0 wl_in1 wl_in2 wl_in3 wg_in wvo_in x_in0 x_in1 stored
            ident_zero ident_done consts_done adj_off_done wcat_split gate_exp_done gate_den_done
            gate_inv_done gate_coef_done tri_done u_done u_diag_done u_hi_done u_lo_done m_done m_hi_done m_lo_done
            stats1 aggr1 var1 rstd1 shift1 h_done h_hi_done h_lo_done
            gt_done gt_hi_done qk_done gt_lo_done q_top_done q_row_done q_max_done cols_done
            exps_done r_row_done r_copied pw_done pw_hi_done pw_lo_done
            yt_done rinv_done yt_scaled y_done relu_done x1_done
            stats2 aggr2 var2 rstd2 shift2 h2_done h2t_done h2t_hi_done h2t_lo_done
            tl_done tl_hi_done tl_lo_done tg_done tg_hi_done tg_lo_done
            wv_hi_done wv_lo_done wo_hi_done wo_lo_done
            s_done s_copied s_turned gram_done sq_done guard_done rnorm_done norm_row_done norm_copied
            al_done dist_done dist2_done ag_done kl_done kg_done scale_done deg_done
            deg_guard_done deg_inv_done row_coef_done kg_scaled_done k_done
            kt_done kt_hi_done kt_lo_done v_done v_hi_done v_lo_done out_done added""".split()
        s = namedtuple("Semaphores", names)(*[sem(n) for n in names])
        x_in = [s.x_in0, s.x_in1]
        wl_in = [s.wl_in0, s.wl_in1, s.wl_in2, s.wl_in3]

        block = ctx.enter_context(nc.Block())
        TURNS = (B - 4) // 2

        def batch(n):
            return Batch(n, n % 2, n // 2)

        def v_tile(b, r):
            return b.p if r == 0 else 2

        def u_parts(u, d):
            return (2 * FT - 1) * u + min(2 * d + 2, 2 * FT - 1)

        def f(t):
            return t.bitcast(f32)

        @block.sync
        def _(sp):
            def load_x(b):
                sp.dma_start(xt[b.p][:, :, :], x_v[b.n]).then_inc(x_in[b.p], 16)

            def load_next_x(b):
                sp.wait_ge(s.x1_done, RT * (b.n + 1))
                load_x(after(b, 2))

            def store(b):
                sp.wait_ge(s.added, RT * (b.n + 1))
                sp.dma_start(out_v[b.n], result[:, :, :]).then_inc(s.stored, 16)

            for k in range(FT):
                sp.dma_start(stage_a[:, k, :], wl[k * P:(k + 1) * P, :]).then_inc(wl_in[k], 16)
            load_x(Batch(0, 0, 0))
            sp.dma_start(wcat[:, :, :], adj_wq_wk.rearrange("(r p) o -> p r o", p=P)).then_inc(s.weights_in, 16)
            sp.dma_start(bm_col[:, :], bm.rearrange("(r p) -> p r", p=P),
                         allow_slow_non_contiguous=True).then_inc(s.small_in, 16)
            sp.dma_start(stage_b[:, :, :], wg.rearrange("(t p) d -> p t d", p=P)).then_inc(s.wg_in, 16)
            sp.dma_start(gate_in[:, 0:1], gate_logit.partition_broadcast(P)).then_inc(s.small_in, 16)
            sp.dma_start(gate_in[:, 1:2], log_sigma.partition_broadcast(P)).then_inc(s.small_in, 16)
            for i, stage in enumerate(wv_stage):
                sp.dma_start(stage[:, :, :],
                             wv.rearrange("(t p) d -> p t d", p=P)[:, 2 * i:2 * i + 2, :]).then_inc(s.wvo_in, 16)
            for k, stage in enumerate(wo_stage):
                sp.dma_start(stage, wo_t[k * P:(k + 1) * P, :]).then_inc(s.wvo_in, 16)
            load_x(Batch(1, 1, 0))
            sp.dma_start(adj_off[:, :, :], adj.rearrange("(r p) m -> p r m", p=P)).then_inc(s.adj_in, 16)
            for n in range(2):
                load_next_x(batch(n))
            with sp.Fori(0, TURNS) as i:
                for k in (1, 2):
                    b = Batch(2 * i + k, k % 2, i + k // 2)
                    store(after(b, -1))
                    load_next_x(after(b, 1))
            for n in range(2 * TURNS, B - 1):
                store(batch(n))
            for r in range(RT):
                sp.wait_ge(s.added, RT * (B - 1) + r + 1)
                sp.dma_start(out_v[B - 1][:, r, :], result[:, r, :]).then_inc(s.stored, 16)
            sp.wait_ge(s.stored, 1 + 16 * (B - 1 + RT))

        def run_batches(eng, turn, last_turn):
            turn(batch(0), True, False)
            with eng.Fori(0, TURNS) as i:
                for k in (1, 2):
                    turn(Batch(2 * i + k, k % 2, i + k // 2), True, True)
            for n in range(2 * TURNS + 1, B - 1):
                turn(batch(n), n + 2 < B, True)
            last_turn(batch(B - 1), batch(B - 2))

        FIRST = batch(0)

        @block.tensor
        def _(pe):
            def product(dst, pairs, starts=True, ends=True):
                last = None
                for n, (lh, ll, rh, rl) in enumerate(pairs):
                    nc.tensor.matmul(dst, lh, rh, start=(starts and n == 0), stop=False)
                    nc.tensor.matmul(dst, lh, rl, start=False, stop=False)
                    last = nc.tensor.matmul(dst, ll, rh, start=False, stop=(ends and n == len(pairs) - 1))
                return last

            def row_of(dst, col):
                return nc.tensor.matmul(dst, col.broadcast_to((P, P)), ident[:, :], is_transpose=True,
                                        start=True, stop=True)

            def adj_h(c, values_before):
                pe.wait_ge(s.h_hi_done, c.n + 1)
                pe.wait_ge(s.h_lo_done, RT * (c.n + 1))
                for j in range(FT):
                    if values_before and j == 2:
                        pe.wait_ge(s.v_lo_done, RT * (c.n - 1))
                    if values_before and j == FT - 1:
                        pe.wait_ge(s.norm_copied, c.n - 1)
                    js = slice(j * P, (j + 1) * P)
                    product(bank[GT_BANK[j]][:, 0:CQ],
                            [(h_hi[:, r, js], h_lo[:, r, js], wcat_hi[:, r, :], wcat_lo[:, r, :])
                             for r in range(RT)]).then_inc(s.gt_done, 1)

            def max_q(c):
                pe.wait_ge(s.q_top_done, c.n + 1)
                pe.wait_ge(s.gt_lo_done, FT * (c.n + 1))
                row_of(bank[ROW_BANK][:, 0:P], q_top[:, 0:1]).then_inc(s.q_row_done, 1)

            def rows_r(c):
                pe.wait_ge(s.exps_done, 3 * (c.n + 1))
                for j in range(FT):
                    last = row_of(bank[ROW_BANK][:, j * P:(j + 1) * P], r_col[:, j:j + 1])
                last.then_inc(s.r_row_done, 1)

            def weighted(c, tiles):
                for j in range(FT):
                    pe.wait_ge(s.pw_hi_done, FT * c.n + j + 1)
                    pe.wait_ge(s.pw_lo_done, FT * c.n + j + 1)
                    for m in tiles:
                        ms = slice(m * P, (m + 1) * P)
                        dst = bank[YT_BANK[m]][:, 0:C + 2]
                        nc.tensor.matmul(dst, pw_hi[:, j, ms], gt_hi[:, j, :], start=(j == 0), stop=False)
                        nc.tensor.matmul(dst, pw_hi[:, j, ms], gt_lo[:, j, :], start=False, stop=False)
                        last = nc.tensor.matmul(dst, pw_lo[:, j, ms], gt_hi[:, j, :], start=False, stop=(j == FT - 1))
                        if j == FT - 1:
                            last.then_inc(s.yt_done, 1)

            def transpose_y(c):
                pe.wait_ge(s.yt_scaled, FT * (c.n + 1))
                for r in range(RT):
                    for m in range(FT):
                        last = nc.tensor.transpose(bank[Y_BANK[r]][:, m * P:(m + 1) * P],
                                                   yt[:, m, r * P:(r + 1) * P], ident[:, :])
                    last.then_inc(s.y_done, 1)

            def transpose_h2(c):
                pe.wait_ge(s.h2_done, RT * (c.n + 1))
                for half in range(2):
                    for t in range(2):
                        for r in range(RT):
                            d = 2 * half + t
                            last = nc.tensor.transpose(bank[H2T_BANK[half]][:, t * C + r * P:t * C + (r + 1) * P],
                                                       h2[:, r, d * P:(d + 1) * P], ident[:, :])
                    last.then_inc(s.h2t_done, 1)

            def project(u_hi, u_lo, done, banks, tiles):
                for e in tiles:
                    es = slice(e * P, (e + 1) * P)
                    last = product(bank[banks[e // 2]][:, (e % 2) * C:(e % 2 + 1) * C],
                                   [(u_hi[:, d, es], u_lo[:, d, es], h2t_hi[:, d, :], h2t_lo[:, d, :])
                                    for d in range(e + 1)])
                last.then_inc(done, 1)

            def half_gram(r, first=0, end=FT):
                rs = slice(r * P, (r + 1) * P)
                last = product(bank[S_BANK[r]][:, :],
                               [(h2t_hi[:, d, rs], h2t_lo[:, d, rs], both_kinds(t_hi, d), both_kinds(t_lo, d))
                                for d in range(first, end)], first == 0, end == FT)
                if end == FT:
                    last.then_inc(s.s_done, 1)

            def turn_over(b):
                for r in range(RT):
                    for m in range(RT):
                        if r == 0:
                            pe.wait_ge(s.s_copied, RT * b.n + m + 1)
                        for k in range(2):
                            at = k * C + m * P
                            last = nc.tensor.transpose(bank[S_BANK[r]][:, at:at + P],
                                                       s_rows[:, m, k * C + r * P:k * C + (r + 1) * P], ident[:, :])
                    last.then_inc(s.s_turned, 1)

            def rows_norms(b):
                pe.wait_ge(s.rnorm_done, b.n + 1)
                pe.wait_ge(s.sq_done, 4 * (b.n + 1))
                for r in range(RT):
                    row_of(bank[ROW_BANK][:, r * P:(r + 1) * P], rnorm[:, r:r + 1])
                for r in range(RT):
                    last = row_of(bank[ROW_BANK][:, C + r * P:C + (r + 1) * P], sq[:, 1, r:r + 1])
                last.then_inc(s.norm_row_done, 1)

            def values(b, r, first=0, end=FT):
                rs = slice(r * P, (r + 1) * P)
                last = product(bank[V_BANK[r]][:, :],
                               [(h2t_hi[:, d, rs], h2t_lo[:, d, rs], m_hi[:, d, :], m_lo[:, d, :])
                                for d in range(first, end)], first == 0, end == FT)
                if end == FT:
                    last.then_inc(s.v_done, 1)

            def transpose_k(b):
                pe.wait_ge(s.k_done, RT * (b.n + 1))
                for m in range(RT):
                    for r in range(RT):
                        last = nc.tensor.transpose(bank[KT_BANK][:, m * C + r * P:m * C + (r + 1) * P],
                                                   kmat[:, r, m * P:(m + 1) * P], ident[:, :])
                last.then_inc(s.kt_done, 1)

            def mix(b, r, banks):
                rs = slice(r * P, (r + 1) * P)
                product(bank[banks[r]][:, :],
                        [(kt_hi[:, m, rs], kt_lo[:, m, rs], v_hi[v_tile(b, m)][:, :], v_lo[v_tile(b, m)][:, :])
                         for m in range(RT)]).then_inc(s.out_done, 1)

            def make_u(u, stage, d):
                if u == 1:
                    pe.wait_ge(s.u_lo_done, u_parts(0, d))
                for k in range(FT):
                    if u == 0 and d == 0:
                        pe.wait_ge(wl_in[k], 16)
                    last = nc.tensor.matmul(bank[U_BANK[d]][:, d * P:N], stage[:, k, d * P:(d + 1) * P],
                                            stage[:, k, d * P:N], start=(k == 0), stop=(k == FT - 1))
                last.then_inc(s.u_done, 1)

            def make_m(d):
                if d >= 2:
                    pe.wait_ge(s.u_lo_done, u_parts(1, d))
                ds = slice(d * P, (d + 1) * P)
                product(bank[M_BANK[d]][:, :],
                        [(wv_hi[k][:, ds], wv_lo[k][:, ds], wo_hi[k], wo_lo[k])
                         for k in range(FT)]).then_inc(s.m_done, 1)

            for d in range(FT):
                make_u(0, stage_a, d)
            pe.wait_ge(s.ident_done, 1)
            pe.wait_ge(s.consts_done, 2)
            pe.wait_ge(s.wcat_split, 2)
            adj_h(FIRST, False)
            pe.wait_ge(s.wg_in, 16)
            make_u(1, stage_b, 0)
            max_q(FIRST)
            make_u(1, stage_b, 1)
            rows_r(FIRST)
            make_u(1, stage_b, 2)
            make_u(1, stage_b, 3)
            pe.wait_ge(s.u_lo_done, u_parts(1, 1))
            weighted(FIRST, (0, 1))
            weighted(FIRST, (2,))
            weighted(FIRST, (3,))
            pe.wait_ge(s.wv_lo_done, FT)
            pe.wait_ge(s.wo_lo_done, FT)
            make_m(0)
            transpose_y(FIRST)
            make_m(1)
            make_m(2)
            make_m(3)
            transpose_h2(FIRST)

            def turn(b, _, finish):
                c, e = after(b, 1), after(b, -1)
                if not finish:
                    pe.wait_ge(s.m_lo_done, 2)
                adj_h(c, finish)
                pe.wait_ge(s.h2t_hi_done, 2 * (b.n + 1))
                pe.wait_ge(s.h2t_lo_done, 2 * (b.n + 1))
                if not finish:
                    pe.wait_ge(s.m_lo_done, FT)
                pe.wait_ge(s.gt_lo_done, FT * c.n + 2)
                values(b, 0)
                max_q(c)
                project(ul_hi, ul_lo, s.tl_done, TL_BANK, (0, 1))
                project(ul_hi, ul_lo, s.tl_done, TL_BANK, (2, 3))
                rows_r(c)
                pe.wait_ge(s.v_lo_done, RT * b.n + 1)
                project(ug_hi, ug_lo, s.tg_done, TG_BANK, (0, 1))
                if finish:
                    transpose_k(e)
                project(ug_hi, ug_lo, s.tg_done, TG_BANK, (2, 3))
                if finish:
                    pe.wait_ge(s.kt_lo_done, b.n)
                    pe.wait_ge(s.v_lo_done, RT * b.n)
                    mix(e, 0, OUT_BANK)
                    mix(e, 1, OUT_BANK)
                pe.wait_ge(s.tl_lo_done, 2 * (b.n + 1))
                weighted(c, (0, 1))
                weighted(c, (2,))
                weighted(c, (3,))
                if finish:
                    pe.wait_ge(s.added, RT * b.n)
                pe.wait_ge(s.tg_lo_done, 2 * (b.n + 1))
                half_gram(0, 0, FT // 2)
                transpose_y(c)
                half_gram(0, FT // 2, FT)
                half_gram(1)
                values(b, 1, 0, 1)
                turn_over(b)
                values(b, 1, 1, FT)
                transpose_h2(c)
                rows_norms(b)

            def last_turn(b, e):
                pe.wait_ge(s.h2t_hi_done, 2 * (b.n + 1))
                pe.wait_ge(s.h2t_lo_done, 2 * (b.n + 1))
                project(ul_hi, ul_lo, s.tl_done, TL_BANK, (0, 1))
                project(ul_hi, ul_lo, s.tl_done, TL_BANK, (2, 3))
                pe.wait_ge(s.v_lo_done, RT * b.n)
                project(ug_hi, ug_lo, s.tg_done, TG_BANK, (0, 1))
                project(ug_hi, ug_lo, s.tg_done, TG_BANK, (2, 3))
                pe.wait_ge(s.gram_done, RT * b.n)
                pe.wait_ge(s.tl_lo_done, 2 * (b.n + 1))
                pe.wait_ge(s.tg_lo_done, 2 * b.n + 1)
                half_gram(0, 0, FT // 2)
                transpose_k(e)
                pe.wait_ge(s.tg_lo_done, 2 * (b.n + 1))
                half_gram(0, FT // 2, FT)
                half_gram(1)
                values(b, 0, 0, 1)
                turn_over(b)
                pe.wait_ge(s.kt_lo_done, b.n)
                mix(e, 0, LAST_OUT_BANK)
                mix(e, 1, LAST_OUT_BANK)
                rows_norms(b)
                values(b, 0, 1, FT)
                values(b, 1)
                transpose_k(b)
                pe.wait_ge(s.kt_lo_done, B)
                pe.wait_ge(s.v_lo_done, RT * B)
                mix(b, 0, OUT_BANK)
                mix(b, 1, OUT_BANK)

            run_batches(pe, turn, last_turn)

        @block.scalar
        def _(act):
            def normalised(b, src, done, which, ready):
                act.wait_ge(ready, b.n + 1)
                for r in range(RT):
                    nc.scalar.activation(done[0][:, r, :], src[:, r, :], ACT.Relu,
                                         bias=shift[:, which, r:r + 1],
                                         scale=rstd[:, which, r:r + 1]).then_inc(done[1], 1)

            def high_h(a):
                act.wait_ge(s.h_done, RT * (a.n + 1))
                nc.scalar.copy(h_hi[:, :, :], h[:, :, :]).then_inc(s.h_hi_done, 1)

            def high_gt(c, first, end):
                for j in range(first, end):
                    act.wait_ge(s.gt_done, FT * c.n + j + 1)
                    nc.scalar.copy(gt_hi[:, j, 0:C], bank[GT_BANK[j]][:, 0:C]).then_inc(s.gt_hi_done, 1)

            def exps(c):
                act.wait_ge(s.cols_done, 2 * (c.n + 1))
                nc.scalar.activation(r_col[:, :], cols[:, 1, :], ACT.Exp, bias=neg_shift[:, 0:1],
                                     scale=1 - SLOPE).then_inc(s.exps_done, 1)
                nc.scalar.activation(a_col[:, :], cols[:, 0, :], ACT.Exp).then_inc(s.exps_done, 1)
                nc.scalar.activation(b_col[:, :], cols[:, 0, :], ACT.Exp, bias=neg_shift[:, 0:1],
                                     scale=SLOPE).then_inc(s.exps_done, 1)

            def copy_r(c):
                act.wait_ge(s.r_row_done, c.n + 1)
                nc.scalar.copy(r_row[:, :], bank[ROW_BANK][:, :]).then_inc(s.r_copied, 1)

            def high_pw(c):
                for j in range(FT):
                    act.wait_ge(s.pw_done, FT * c.n + j + 1)
                    nc.scalar.copy(pw_hi[:, j, :], pw[:, j, :]).then_inc(s.pw_hi_done, 1)

            def scale_y(c, m):
                act.wait_ge(s.rinv_done, FT * c.n + m + 1)
                nc.scalar.activation(yt[:, m, :], bank[YT_BANK[m]][:, 0:C], ACT.Copy,
                                     scale=rinv_col[:, m:m + 1]).then_inc(s.yt_scaled, 1)

            def relu_y(c):
                for r in range(RT):
                    act.wait_ge(s.y_done, RT * c.n + r + 1)
                    nc.scalar.activation(yn[:, r, :], bank[Y_BANK[r]][:, :], ACT.Relu,
                                         bias=bm_col[:, r:r + 1]).then_inc(s.relu_done, 1)

            def high(wait_on, count, dst, src, done):
                act.wait_ge(wait_on, count)
                nc.scalar.copy(dst, src).then_inc(done, 1)

            def high_kt(b):
                high(s.kt_done, b.n + 1, kt_hi[:, :, :].rearrange("p r c -> p (r c)"), bank[KT_BANK][:, :],
                     s.kt_hi_done)

            def high_h2t(c):
                for i in range(2):
                    high(s.h2t_done, 2 * c.n + i + 1, two_tiles(h2t_hi, i), bank[H2T_BANK[i]][:, :], s.h2t_hi_done)

            def high_v(b, r):
                high(s.v_done, RT * b.n + r + 1, v_hi[v_tile(b, r)][:, :], bank[V_BANK[r]][:, :], s.v_hi_done)

            def high_m(d):
                high(s.m_done, d + 1, m_hi[:, d, :], bank[M_BANK[d]][:, :], s.m_hi_done)

            def high_wv(k):
                high(s.wvo_in, 96, wv_hi[k], wv_stage[k // 2][:, k % 2, :], s.wv_hi_done)

            def high_u(u, dst, d):
                high(s.u_diag_done, FT * u + d + 1, dst[:, d, d * P:(d + 1) * P], diag[:, d, :], s.u_hi_done)
                if d < FT - 1:
                    nc.scalar.copy(dst[:, d, (d + 1) * P:N],
                                   bank[U_BANK[d]][:, (d + 1) * P:N]).then_inc(s.u_hi_done, 1)

            act.wait_ge(s.consts_done, 2)
            act.wait_ge(s.weights_in, 16)
            nc.scalar.copy(wcat_hi[:, :, :], wcat[:, :, :]).then_inc(s.wcat_split, 1)
            normalised(FIRST, xt[0], (h, s.h_done), 0, s.shift1)
            high_h(FIRST)
            act.wait_ge(s.small_in, 48)
            nc.scalar.activation(gate_exp[:, 0:1], gate_in[:, 0:1], ACT.Exp, scale=-1.0).then_inc(s.gate_exp_done, 1)
            nc.scalar.activation(gate_exp[:, 1:2], gate_in[:, 1:2], ACT.Exp).then_inc(s.gate_exp_done, 1)
            for d in range(FT - 1):
                high_u(0, ul_hi, d)
            high_gt(FIRST, 0, 2)
            high_u(0, ul_hi, FT - 1)
            high_gt(FIRST, 2, FT)
            high_wv(0)
            high_wv(1)
            exps(FIRST)
            high_u(1, ug_hi, 0)
            high_u(1, ug_hi, 1)
            copy_r(FIRST)
            high_pw(FIRST)
            high_wv(2)
            high_wv(3)
            for k in range(FT):
                high(s.wvo_in, 96, wo_hi[k], wo_stage[k], s.wo_hi_done)
            for m in range(FT):
                scale_y(FIRST, m)
            high_u(1, ug_hi, 2)
            high_u(1, ug_hi, 3)
            high_m(0)
            relu_y(FIRST)
            high_m(1)
            normalised(after(FIRST, 1), xt[1], (h, s.h_done), 0, s.shift1)
            high_h(after(FIRST, 1))
            normalised(FIRST, x1[0], (h2, s.h2_done), 1, s.shift2)
            for d in range(2, FT):
                high_m(d)
            high_h2t(FIRST)

            def high_tl(b):
                for i in range(2):
                    high(s.tl_done, 2 * b.n + i + 1, t_hi[:, 2 * i:2 * i + 2, 0, :], in_two(TL_BANK[i]), s.tl_hi_done)

            def high_tg(b):
                for i in range(2):
                    high(s.tg_done, 2 * b.n + i + 1, t_hi[:, 2 * i:2 * i + 2, 1, :], in_two(TG_BANK[i]), s.tg_hi_done)

            def copy_s(b, r):
                high(s.s_done, RT * b.n + r + 1, s_rows[:, r, :], bank[S_BANK[r]][:, :], s.s_copied)

            def copy_norms(b):
                high(s.norm_row_done, b.n + 1, norm_row[:, :, :].rearrange("p s c -> p (s c)"),
                     bank[ROW_BANK][:, :], s.norm_copied)

            def distance_kernel(b):
                act.wait_ge(s.dist2_done, RT * (b.n + 1))
                nc.scalar.activation(ag[:, :, :], dist[:, :, :], ACT.Exp,
                                     scale=gate_inv[:, 1:2]).then_inc(s.ag_done, 1)

            def turn(b, norm0, finish):
                c, a, e = after(b, 1), after(b, 2), after(b, -1)
                high_gt(c, 0, FT)
                if finish:
                    distance_kernel(e)
                high_v(b, 0)
                exps(c)
                high_tl(b)
                copy_r(c)
                if finish:
                    high_kt(e)
                high_pw(c)
                high_tg(b)
                for m in range(FT):
                    scale_y(c, m)
                if norm0:
                    normalised(a, xt[a.p], (h, s.h_done), 0, s.shift1)
                relu_y(c)
                copy_s(b, 0)
                if norm0:
                    high_h(a)
                copy_s(b, 1)
                normalised(c, x1[c.p], (h2, s.h2_done), 1, s.shift2)
                high_v(b, 1)
                high_h2t(c)
                copy_norms(b)

            def last_turn(b, e):
                distance_kernel(e)
                high_tl(b)
                high_tg(b)
                high_kt(e)
                copy_s(b, 0)
                copy_s(b, 1)
                copy_norms(b)
                distance_kernel(b)
                high_v(b, 0)
                high_v(b, 1)
                high_kt(b)

            run_batches(act, turn, last_turn)

        @block.gpsimd
        def _(pool):
            def power(dst, src, ready, count, done):
                pool.wait_ge(ready, count)
                nc.gpsimd.tensor_tensor(dst, src, minus_half[:, :], ALU.pow).then_inc(done, 1)

            nc.gpsimd.memset(minus_half[:, :], -0.5).then_inc(s.consts_done, 1)
            nc.gpsimd.memset(ident[:, :], 0.0).then_inc(s.ident_zero, 1)
            pool.wait_ge(s.ident_zero, 1)
            nc.gpsimd.affine_select(out=ident[:, :], in_=ident[:, :], compare_op=ALU.not_equal, fill=1.0, base=0,
                                    pattern=[[-1, P]], channel_multiplier=1).then_inc(s.ident_done, 1)
            nc.gpsimd.memset(tri[:, :], 1.0).then_inc(s.tri_done, 1)
            pool.wait_ge(s.tri_done, 1)
            nc.gpsimd.affine_select(out=tri[:, :], in_=tri[:, :], compare_op=ALU.is_ge, fill=0.0, base=0,
                                    pattern=[[1, P]], channel_multiplier=-1).then_inc(s.tri_done, 1)
            pool.wait_ge(s.tri_done, 2)
            nc.gpsimd.affine_select(out=tri[:, :], in_=tri[:, :], compare_op=ALU.not_equal, fill=0.5, base=0,
                                    pattern=[[1, P]], channel_multiplier=-1).then_inc(s.tri_done, 1)
            pool.wait_ge(s.consts_done, 2)
            power(rstd[:, 0, :], var_eps[:, 0, :], s.var1, 1, s.rstd1)
            power(rstd[:, 0, :], var_eps[:, 0, :], s.var1, 2, s.rstd1)
            power(rstd[:, 1, :], var_eps[:, 1, :], s.var2, 1, s.rstd2)
            pool.wait_ge(s.adj_in, 16)
            nc.gpsimd.affine_select(out=adj_off[:, :, :], in_=adj_off[:, :, :], compare_op=ALU.not_equal, fill=0.0,
                                    base=0, pattern=[[P, RT], [-1, C]], channel_multiplier=1).then_inc(s.adj_off_done, 1)

            def turn(b, norm0, finish):
                c, a = after(b, 1), after(b, 2)
                if norm0:
                    power(rstd[:, 0, :], var_eps[:, 0, :], s.var1, a.n + 1, s.rstd1)
                power(rstd[:, 1, :], var_eps[:, 1, :], s.var2, c.n + 1, s.rstd2)
                power(rnorm[:, :], sq_guard[:, :], s.guard_done, b.n + 1, s.rnorm_done)

            def last_turn(b, e):
                power(rnorm[:, :], sq_guard[:, :], s.guard_done, b.n + 1, s.rnorm_done)

            run_batches(pool, turn, last_turn)

        @block.vector
        def _(dve):
            def low(wait_on, count, dst, src, hi, done):
                dve.wait_ge(wait_on, count)
                nc.vector.tensor_tensor(dst, src, f(hi), ALU.subtract).then_inc(done, 1)

            def statistics(b, src, which, src_ready, counts, stat_sem):
                for r in range(RT):
                    dve.wait_ge(src_ready, counts[r])
                    nc.vector.bn_stats(stats[:, which, r, :], src[:, r, :]).then_inc(stat_sem, 1)
                dve.wait_ge(stat_sem, RT * (b.n + 1))

            def aggregate(b, which, aggr_sem, var_sem):
                for r in range(RT):
                    nc.vector.bn_aggr(mean_var[:, which, r, :], stats[:, which, r, :]).then_inc(aggr_sem, 1)
                dve.wait_ge(aggr_sem, RT * (b.n + 1))
                nc.vector.tensor_scalar(var_eps[:, which, :], mean_var[:, which, :, 1], LN_EPS, None,
                                        ALU.add).then_inc(var_sem, 1)

            def statistics1(a):
                statistics(a, xt[a.p], 0, x_in[a.p], [16 * (a.half + 1)] * RT, s.stats1)

            def aggregate1(a):
                aggregate(a, 0, s.aggr1, s.var1)

            def statistics2(c):
                statistics(c, x1[c.p], 1, s.x1_done, [RT * c.n + r + 1 for r in range(RT)], s.stats2)

            def aggregate2(c):
                aggregate(c, 1, s.aggr2, s.var2)

            def minus_mean_rstd(b, which, rstd_sem, shift_sem):
                dve.wait_ge(rstd_sem, b.n + 1)
                nc.vector.scalar_tensor_tensor(out=shift[:, which, :], in0=mean_var[:, which, :, 0], scalar=-1.0,
                                               in1=rstd[:, which, :], op0=ALU.mult, op1=ALU.mult).then_inc(shift_sem, 1)

            def low_h(a, r):
                low(s.h_hi_done, a.n + 1, h_lo[:, r, :], h[:, r, :], h_hi[:, r, :], s.h_lo_done)

            def low_gt(c, first, end):
                for j in range(first, end):
                    dve.wait_ge(s.gt_hi_done, FT * c.n + j + 1)
                    nc.vector.tensor_copy(qk[:, j, :], bank[GT_BANK[j]][:, C:CQ]).then_inc(s.qk_done, 1)
                    nc.vector.tensor_tensor(gt_lo[:, j, 0:C], bank[GT_BANK[j]][:, 0:C], f(gt_hi[:, j, 0:C]),
                                            ALU.subtract).then_inc(s.gt_lo_done, 1)

            def top_q(c):
                dve.wait_ge(s.qk_done, FT * (c.n + 1))
                nc.vector.reduce_max(q_top[:, :], qk[:, :, 0], AX_X).then_inc(s.q_top_done, 1)

            def max_of_q(c):
                dve.wait_ge(s.q_row_done, c.n + 1)
                nc.vector.reduce_max(q_max[:, :], bank[ROW_BANK][:, 0:P], AX_X).then_inc(s.q_max_done, 1)

            def columns(c):
                dve.wait_ge(s.q_max_done, c.n + 1)
                nc.vector.tensor_scalar(cols[:, 1, :], qk[:, :, 1], q_max[:, 0:1], T_MAX, ALU.add,
                                        ALU.min).then_inc(s.cols_done, 1)
                nc.vector.tensor_scalar(cols[:, 0, :], qk[:, :, 0], q_max[:, 0:1], None,
                                        ALU.subtract).then_inc(s.cols_done, 1)

            def weights_p(c, first, end):
                dve.wait_ge(s.r_copied, c.n + 1)
                dve.wait_ge(s.exps_done, 3 * (c.n + 1))
                for j in range(first, end):
                    nc.vector.tensor_scalar(pw[:, j, :], r_row[:, :], a_col[:, j:j + 1], b_col[:, j:j + 1],
                                            ALU.mult, ALU.max).then_inc(s.pw_done, 1)

            def low_p(c, first, end):
                for j in range(first, end):
                    low(s.pw_hi_done, FT * c.n + j + 1, pw_lo[:, j, :], pw[:, j, :], pw_hi[:, j, :], s.pw_lo_done)

            def invert_sum(c, m):
                dve.wait_ge(s.yt_done, FT * c.n + m + 1)
                nc.vector.reciprocal(rinv_col[:, m:m + 1], bank[YT_BANK[m]][:, C:C + 1]).then_inc(s.rinv_done, 1)

            def residual(c):
                for r in range(RT):
                    dve.wait_ge(s.relu_done, RT * c.n + r + 1)
                    nc.vector.tensor_tensor(x1[c.p][:, r, :], xt[c.p][:, r, :], yn[:, r, :],
                                            ALU.add).then_inc(s.x1_done, 1)

            def low_h2t(c):
                for i in range(2):
                    low(s.h2t_hi_done, 2 * c.n + i + 1, two_tiles(h2t_lo, i), bank[H2T_BANK[i]][:, :],
                        two_tiles(h2t_hi, i), s.h2t_lo_done)

            def add_transpose(b):
                for r in range(RT):
                    dve.wait_ge(s.s_turned, RT * b.n + r + 1)
                    nc.vector.tensor_tensor(gram[:, r, :], bank[S_BANK[r]][:, :], s_rows[:, r, :],
                                            ALU.add).then_inc(s.gram_done, 1)

            def squared_norms(b, k):
                dve.wait_ge(s.gram_done, RT * (b.n + 1))
                for r in range(RT):
                    at = k * C + r * P
                    nc.vector.tensor_tensor_reduce(
                        out=diag[:, 2 * k + r, :], in0=gram[:, r, at:at + P], in1=ident[:, :], scale=1.0,
                        scalar=0.0, op0=ALU.mult, op1=ALU.add, accum_out=sq[:, k, r:r + 1]).then_inc(s.sq_done, 1)

            def guard_norms(b):
                dve.wait_ge(s.sq_done, 4 * b.n + RT)
                nc.vector.tensor_scalar(sq_guard[:, :], sq[:, 0, :], NORM_EPS * NORM_EPS, None,
                                        ALU.max).then_inc(s.guard_done, 1)

            def kernels(b):
                dve.wait_ge(s.norm_copied, b.n + 1)
                dve.wait_ge(s.sq_done, 4 * (b.n + 1))
                gl, gg = gram[:, :, 0:C], gram[:, :, C:2 * C]
                nc.vector.scalar_tensor_tensor(
                    out=dist[:, :, :], in0=gg, scalar=-2.0, in1=norm_row[:, 1:2, :].broadcast_to((P, RT, C)),
                    op0=ALU.mult, op1=ALU.add).then_inc(s.dist_done, 1)
                nc.vector.scalar_tensor_tensor(
                    out=al[:, :, :], in0=gl, scalar=0.0, in1=norm_row[:, 0:1, :].broadcast_to((P, RT, C)),
                    op0=ALU.max, op1=ALU.mult).then_inc(s.al_done, 1)
                dve.wait_ge(s.dist_done, b.n + 1)
                for r in range(RT):
                    nc.vector.tensor_scalar(dist[:, r, :], dist[:, r, :], sq[:, 1, r:r + 1], 0.0, ALU.add,
                                            ALU.max).then_inc(s.dist2_done, 1)

            def masked(b, src, ready, count, dst, g, done):
                dve.wait_ge(ready, count)
                for r in range(RT):
                    nc.vector.tensor_tensor_reduce(
                        out=dst[:, r, :], in0=src[:, r, :], in1=adj_off[:, r, :], scale=1.0, scalar=0.0,
                        op0=ALU.mult, op1=ALU.add, accum_out=row_sum[:, g, r:r + 1]).then_inc(done, 1)

            def row_scales(b):
                nc.vector.tensor_copy(deg_scale[:, 0, :], rnorm[:, :]).then_inc(s.scale_done, 1)
                nc.vector.tensor_scalar(gate_coef[:, 0, :], rnorm[:, :], gate_inv[:, 0:1], None,
                                        ALU.mult).then_inc(s.scale_done, 1)

            def row_coefs(b):
                dve.wait_ge(s.kl_done, RT * (b.n + 1))
                dve.wait_ge(s.kg_done, RT * (b.n + 1))
                dve.wait_ge(s.scale_done, 2 * (b.n + 1))
                nc.vector.tensor_tensor(deg[:, :, :], row_sum[:, :, :], deg_scale[:, :, :],
                                        ALU.mult).then_inc(s.deg_done, 1)
                dve.wait_ge(s.deg_done, b.n + 1)
                nc.vector.tensor_scalar(deg_guard[:, :, :], deg[:, :, :], DEG_EPS, None,
                                        ALU.max).then_inc(s.deg_guard_done, 1)
                dve.wait_ge(s.deg_guard_done, b.n + 1)
                nc.vector.reciprocal(deg_inv[:, :, :], deg_guard[:, :, :]).then_inc(s.deg_inv_done, 1)
                dve.wait_ge(s.deg_inv_done, b.n + 1)
                nc.vector.tensor_tensor(row_coef[:, :, :], deg_inv[:, :, :], gate_coef[:, :, :],
                                        ALU.mult).then_inc(s.row_coef_done, 1)

            def combine(b):
                dve.wait_ge(s.row_coef_done, b.n + 1)
                for r in range(RT):
                    nc.vector.tensor_scalar(dist[:, r, :], kg[:, r, :], row_coef[:, 1, r:r + 1], None,
                                            ALU.mult).then_inc(s.kg_scaled_done, 1)
                for r in range(RT):
                    dve.wait_ge(s.kg_scaled_done, RT * b.n + r + 1)
                    nc.vector.scalar_tensor_tensor(
                        out=kmat[:, r, :], in0=kl[:, r, :], scalar=row_coef[:, 0, r:r + 1], in1=dist[:, r, :],
                        op0=ALU.mult, op1=ALU.add).then_inc(s.k_done, 1)

            def low_v(b, r):
                i = v_tile(b, r)
                low(s.v_hi_done, RT * b.n + r + 1, v_lo[i][:, :], bank[V_BANK[r]][:, :], v_hi[i][:, :], s.v_lo_done)

            def low_kt(b):
                low(s.kt_hi_done, b.n + 1, kt_lo[:, :, :].rearrange("p r c -> p (r c)"), bank[KT_BANK][:, :],
                    kt_hi[:, :, :].rearrange("p r c -> p (r c)"), s.kt_lo_done)

            def add_result(b, r, banks):
                dve.wait_ge(s.stored, 1 + 16 * b.n)
                dve.wait_ge(s.out_done, RT * b.n + r + 1)
                nc.vector.tensor_tensor(result[:, r, :], bank[banks[r]][:, :], x1[b.p][:, r, :],
                                        ALU.add).then_inc(s.added, 1)

            def low_m(d):
                low(s.m_hi_done, d + 1, m_lo[:, d, :], bank[M_BANK[d]][:, :], m_hi[:, d, :], s.m_lo_done)

            def mask_u(u, d):
                dve.wait_ge(s.u_done, FT * u + d + 1)
                nc.vector.tensor_tensor(diag[:, d, :], bank[U_BANK[d]][:, d * P:(d + 1) * P], tri[:, :],
                                        ALU.mult).then_inc(s.u_diag_done, 1)

            def low_u(u, hi, lo, d):
                low(s.u_hi_done, u_parts(u, d), lo[:, d, d * P:(d + 1) * P], diag[:, d, :], hi[:, d, d * P:(d + 1) * P],
                    s.u_lo_done)
                if d < FT - 1:
                    low(s.u_hi_done, u_parts(u, d), lo[:, d, (d + 1) * P:N], bank[U_BANK[d]][:, (d + 1) * P:N],
                        hi[:, d, (d + 1) * P:N], s.u_lo_done)

            def low_wv(k):
                low(s.wv_hi_done, k + 1, wv_lo[k], wv_stage[k // 2][:, k % 2, :], wv_hi[k], s.wv_lo_done)

            nc.vector.memset(neg_shift[:, :], -SHIFT).then_inc(s.stored, 1)
            nc.vector.memset(deg_scale[:, 1, :], 1.0)
            nc.vector.memset(f(gt_hi[:, :, C:C + 2]), 1.0)
            nc.vector.memset(f(gt_lo[:, :, C:C + 2]), 0.0).then_inc(s.consts_done, 1)
            dve.wait_ge(s.consts_done, 2)
            statistics1(FIRST)
            aggregate1(FIRST)
            minus_mean_rstd(FIRST, 0, s.rstd1, s.shift1)
            low(s.wcat_split, 1, wcat_lo[:, :, :], wcat[:, :, :], wcat_hi[:, :, :], s.wcat_split)
            dve.wait_ge(s.tri_done, 3)
            mask_u(0, 0)
            mask_u(0, 1)
            low_h(FIRST, 0)
            low_h(FIRST, 1)
            low_u(0, ul_hi, ul_lo, 0)
            dve.wait_ge(s.gate_exp_done, 2)
            nc.vector.tensor_scalar(gate_den[:, 0:1], gate_exp[:, 0:1], 1.0, None,
                                    ALU.add).then_inc(s.gate_den_done, 1)
            nc.vector.tensor_scalar(gate_den[:, 1:2], gate_exp[:, 1:2], gate_exp[:, 1:2], -2.0, ALU.mult,
                                    ALU.mult).then_inc(s.gate_den_done, 1)
            dve.wait_ge(s.gate_den_done, 2)
            nc.vector.reciprocal(gate_inv[:, :], gate_den[:, :]).then_inc(s.gate_inv_done, 1)
            dve.wait_ge(s.gate_inv_done, 1)
            for r in range(RT):
                nc.vector.tensor_scalar(gate_coef[:, 1, r:r + 1], gate_inv[:, 0:1], -1.0, 1.0, ALU.mult,
                                        ALU.add).then_inc(s.gate_coef_done, 1)
            for d in range(1, FT - 1):
                mask_u(0, d + 1)
                low_u(0, ul_hi, ul_lo, d)
            low_gt(FIRST, 0, 2)
            low_u(0, ul_hi, ul_lo, FT - 1)
            low_gt(FIRST, 2, FT)
            top_q(FIRST)
            low_wv(0)
            low_wv(1)
            max_of_q(FIRST)
            columns(FIRST)
            mask_u(1, 0)
            low_u(1, ug_hi, ug_lo, 0)
            mask_u(1, 1)
            low_u(1, ug_hi, ug_lo, 1)
            weights_p(FIRST, 0, 1)
            for j in range(1, FT):
                weights_p(FIRST, j, j + 1)
                low_p(FIRST, j - 1, j)
            low_p(FIRST, FT - 1, FT)
            low_wv(2)
            low_wv(3)
            for k in range(FT):
                low(s.wo_hi_done, k + 1, wo_lo[k], wo_stage[k], wo_hi[k], s.wo_lo_done)
            for m in range(FT):
                invert_sum(FIRST, m)
            mask_u(1, 2)
            mask_u(1, 3)
            statistics1(after(FIRST, 1))
            low_u(1, ug_hi, ug_lo, 2)
            low_u(1, ug_hi, ug_lo, 3)
            aggregate1(after(FIRST, 1))
            low_m(0)
            minus_mean_rstd(after(FIRST, 1), 0, s.rstd1, s.shift1)
            residual(FIRST)
            statistics2(FIRST)
            aggregate2(FIRST)
            minus_mean_rstd(FIRST, 1, s.rstd2, s.shift2)
            low_m(1)
            low_h(after(FIRST, 1), 0)
            low_h(after(FIRST, 1), 1)
            for d in range(2, FT):
                low_m(d)
            low_h2t(FIRST)
            dve.wait_ge(s.adj_off_done, 1)
            dve.wait_ge(s.gate_coef_done, 2)

            def low_tl(b):
                for i in range(2):
                    low(s.tl_hi_done, 2 * b.n + i + 1, t_lo[:, 2 * i:2 * i + 2, 0, :], in_two(TL_BANK[i]),
                        t_hi[:, 2 * i:2 * i + 2, 0, :], s.tl_lo_done)

            def low_tg(b, i):
                low(s.tg_hi_done, 2 * b.n + i + 1, t_lo[:, 2 * i:2 * i + 2, 1, :], in_two(TG_BANK[i]),
                    t_hi[:, 2 * i:2 * i + 2, 1, :], s.tg_lo_done)

            def masked_kernels(b):
                masked(b, al, s.al_done, b.n + 1, kl, 0, s.kl_done)
                masked(b, ag, s.ag_done, b.n + 1, kg, 1, s.kg_done)

            def turn(b, norm0, finish):
                c, a, e = after(b, 1), after(b, 2), after(b, -1)
                low_gt(c, 0, FT // 2)
                if finish:
                    kernels(e)
                low_gt(c, FT // 2, FT)
                top_q(c)
                if finish:
                    masked_kernels(e)
                max_of_q(c)
                if finish:
                    row_scales(e)
                columns(c)
                low_v(b, 0)
                if finish:
                    row_coefs(e)
                    combine(e)
                low_tl(b)
                weights_p(c, 0, FT // 2)
                if finish:
                    low_kt(e)
                weights_p(c, FT // 2, FT)
                low_p(c, 0, FT)
                if norm0:
                    statistics1(a)
                low_tg(b, 0)
                if norm0:
                    aggregate1(a)
                low_tg(b, 1)
                if norm0:
                    minus_mean_rstd(a, 0, s.rstd1, s.shift1)
                invert_sum(c, 0)
                invert_sum(c, 1)
                if finish:
                    add_result(e, 0, OUT_BANK)
                    add_result(e, 1, OUT_BANK)
                invert_sum(c, 2)
                invert_sum(c, 3)
                residual(c)
                statistics2(c)
                if norm0:
                    low_h(a, 0)
                aggregate2(c)
                if norm0:
                    low_h(a, 1)
                minus_mean_rstd(c, 1, s.rstd2, s.shift2)
                add_transpose(b)
                squared_norms(b, 0)
                guard_norms(b)
                squared_norms(b, 1)
                low_v(b, 1)
                low_h2t(c)

            def last_turn(b, e):
                kernels(e)
                masked_kernels(e)
                row_scales(e)
                row_coefs(e)
                low_tl(b)
                low_tg(b, 0)
                combine(e)
                low_tg(b, 1)
                low_kt(e)
                add_transpose(b)
                squared_norms(b, 0)
                guard_norms(b)
                squared_norms(b, 1)
                add_result(e, 0, LAST_OUT_BANK)
                add_result(e, 1, LAST_OUT_BANK)
                kernels(b)
                masked_kernels(b)
                row_scales(b)
                row_coefs(b)
                combine(b)
                low_v(b, 0)
                low_v(b, 1)
                low_kt(b)
                add_result(b, 0, OUT_BANK)
                add_result(b, 1, OUT_BANK)

            run_batches(dve, turn, last_turn)


def kernel(**inputs):
    import numpy as np
    import concourse.bacc as bacc
    from concourse import mybir as mb
    from concourse.bass_utils import run_bass_kernel_spmd

    given = {name: np.asarray(a) for name, a in inputs.items()}
    laid = {
        "x": given["x"],
        "adj": given["adj"],
        "adj_wq_wk": np.concatenate([given["adj"].T, given["L0_gnn_wq"][:, None], given["L0_gnn_wk"][:, None]], axis=1),
        "bm": given["L0_gnn_bm"],
        "wl": given["L1_gnn_W_lang"],
        "wg": given["L1_gnn_W_grav"],
        "wv": given["L1_gnn_W_V"],
        "wo_t": given["L1_gnn_W_O"].T,
        "gate_logit": given["L1_gnn_gate_logit"].reshape(1),
        "log_sigma": given["L1_gnn_log_sigma"].reshape(1),
    }
    nc = bacc.Bacc("TRN2", target_bir_lowering=False, num_devices=1)
    arrays, args = {}, []
    for name, a in laid.items():
        arrays[f"in_{name}"] = np.ascontiguousarray(a)
        args.append(nc.dram_tensor(f"in_{name}", a.shape, mb.dt.from_np(a.dtype), kind="ExternalInput").ap())
    args.append(nc.dram_tensor("out_x", given["x"].shape, mb.dt.float32, kind="ExternalOutput").ap())
    graph_layers_kernel(nc, *args)
    r = run_bass_kernel_spmd(nc, [arrays], core_ids=[0])
    return r.results[0]["out_x"]
```
